# Optimizing a Trainium2 kernel written in Bass

```python
import numpy as np
import jax
import jax.numpy as jnp

def _softmax(x, axis=-1):
    return jax.nn.softmax(x, axis=axis)

def _gelu(x):
    return jax.nn.gelu(x, approximate=True)

def _silu(x):
    return jax.nn.silu(x)

def _sigmoid(x):
    return jax.nn.sigmoid(x)

def _layernorm(x, axis=-1, eps=1e-05):
    m = jnp.mean(x, axis=axis, keepdims=True)
    v = jnp.var(x, axis=axis, keepdims=True)
    return (x - m) / jnp.sqrt(v + eps)

def _scatter_add(tgt, idx, src, axis=0):
    return tgt.at[idx].add(src)

def _segment_sum(src, seg, n):
    return jax.ops.segment_sum(src, seg, n)
kernel_name = 'mk_prb_d2_jaxref_r8_5c1fb0'

def setup_inputs(seed: int=0):
    np.random.seed(seed)
    _w = jnp.asarray

    def _L0_attn_setup():
        import jax, jax.numpy as jnp
        import numpy as np
        B, S, E, H, M = (4, 256, 128, 16, 32)
        D = E // H
        LN_EPS = 1e-06

        def softmax_kernel(x, proj):
            x = x * (1.0 / jnp.sqrt(jnp.asarray(x.shape[-1], x.dtype)))
            mapping = jnp.einsum('bhsd,md->bhsm', x, proj)
            correction = jnp.sum(x * x, axis=-1, keepdims=True) * 0.5
            scaling = 1.0 / jnp.sqrt(jnp.asarray(proj.shape[0], x.dtype))
            return scaling * jnp.exp(mapping - correction)

        def favor_forward(x, q_w, q_b, k_w, k_b, v_w, v_b, out_w, out_b, proj, gamma, beta):
            b, s, e = x.shape
            split = lambda y: y.reshape(b, s, H, D).transpose(0, 2, 1, 3)
            Q = split(x @ q_w + q_b)
            K = split(x @ k_w + k_b)
            V = split(x @ v_w + v_b)
            qp = softmax_kernel(Q, proj).transpose(2, 0, 1, 3)
            kp = softmax_kernel(K, proj).transpose(2, 0, 1, 3)
            vs = V.transpose(2, 0, 1, 3)

            def step(carry, inp):
                ksum, kv = carry
                q, k, v = inp
                ksum = ksum + k
                kv = kv + k[..., :, None] * v[..., None, :]
                num = jnp.einsum('bhmd,bhm->bhd', kv, q)
                den = jnp.einsum('bhm,bhm->bh', q, ksum)
                return ((ksum, kv), (num, den))
            init = (jnp.zeros((b, H, M), x.dtype), jnp.zeros((b, H, M, D), x.dtype))
            _, (num, den) = jax.lax.scan(step, init, (qp, kp, vs))
            attn = num / den[..., None]
            attn = attn.transpose(1, 0, 2, 3).reshape(b, s, e)
            main = attn @ out_w + out_b
            res = main + x
            mu = jnp.mean(res, axis=-1, keepdims=True)
            var = jnp.mean(jnp.square(res - mu), axis=-1, keepdims=True)
            return gamma * (res - mu) * jax.lax.rsqrt(var + LN_EPS) + beta
        key = jax.random.key(seed)
        ks = jax.random.split(key, 7)
        glorot = lambda k, sh: jax.random.uniform(k, sh, jnp.float32, -1.0, 1.0) * np.sqrt(6.0 / (sh[0] + sh[1]))
        return {'x': jax.random.normal(ks[0], (B, S, E), jnp.float32), 'q_w': glorot(ks[1], (E, E)), 'q_b': jnp.zeros((E,), jnp.float32), 'k_w': glorot(ks[2], (E, E)), 'k_b': jnp.zeros((E,), jnp.float32), 'v_w': glorot(ks[3], (E, E)), 'v_b': jnp.zeros((E,), jnp.float32), 'out_w': glorot(ks[4], (E, E)), 'out_b': jnp.zeros((E,), jnp.float32), 'proj': jax.random.normal(ks[5], (M, D), jnp.float32), 'gamma': jnp.ones((E,), jnp.float32), 'beta': jnp.zeros((E,), jnp.float32)}
    _L0_attn_in = _L0_attn_setup()

    def _L0_ffn_setup():
        import jax, jax.numpy as jnp
        import numpy as np
        DIM = 128
        DEPTH = 2
        HEADS = 8
        DIM_HEAD = 64
        WINDOW = 64
        INNER = HEADS * DIM_HEAD
        HID = int(DIM * 4 * 2 / 3)
        B, N = (2, 1024)
        QK_SCALE = 8.0

        def shift_token(t):
            t1, t2 = jnp.split(t, 2, axis=-1)
            t2 = jnp.pad(t2, ((0, 0), (1, 0), (0, 0)))[:, :-1]
            return jnp.concatenate([t1, t2], axis=-1)

        def l2norm(t):
            return t / jnp.clip(jnp.linalg.norm(t, axis=-1, keepdims=True), 1e-12)

        def rotate_half(x):
            x1, x2 = jnp.split(x, 2, axis=-1)
            return jnp.concatenate([-x2, x1], axis=-1)

        def rotary_xpos(q, k):
            n = q.shape[-2]
            half_idx = jnp.arange(0, DIM_HEAD, 2, dtype=jnp.float32)
            inv_freq = 1.0 / 10000.0 ** (half_idx / DIM_HEAD)
            t = jnp.arange(n, dtype=jnp.float32)
            freqs = t[:, None] * inv_freq[None, :]
            freqs = jnp.concatenate([freqs, freqs], axis=-1)
            base = (half_idx + 0.4 * DIM_HEAD) / (1.4 * DIM_HEAD)
            power = (t - n // 2) / float(WINDOW // 2)
            scale = base[None, :] ** power[:, None]
            scale = jnp.concatenate([scale, scale], axis=-1)
            cos, sin = (jnp.cos(freqs), jnp.sin(freqs))
            q = q * cos * scale + rotate_half(q) * sin * scale
            k = k * cos / scale + rotate_half(k) * sin / scale
            return (q, k)

        def local_attention(q, k, v):
            b, h, n, d = q.shape
            w = n // WINDOW
            bq = q.reshape(b, h, w, WINDOW, d) * QK_SCALE
            bk = k.reshape(b, h, w, WINDOW, d)
            bv = v.reshape(b, h, w, WINDOW, d)

            def look_around(t):
                p = jnp.pad(t, ((0, 0), (0, 0), (1, 0), (0, 0), (0, 0)))
                return jnp.concatenate([p[:, :, :w], p[:, :, 1:]], axis=3)
            bk, bv = (look_around(bk), look_around(bv))
            bt = jnp.arange(n).reshape(w, WINDOW)
            btp = jnp.pad(bt, ((1, 0), (0, 0)), constant_values=-1)
            btk = jnp.concatenate([btp[:w], btp[1:]], axis=1)
            sim = jnp.einsum('bhwid,bhwjd->bhwij', bq, bk)
            i = bt[:, :, None]
            j = btk[:, None, :]
            mask = (i < j) | (i > j + WINDOW) | (j == -1)
            sim = jnp.where(mask, -jnp.finfo(sim.dtype).max, sim)
            attn = jax.nn.softmax(sim, axis=-1)
            out = jnp.einsum('bhwij,bhwjd->bhwid', attn, bv)
            return out.reshape(b, h, n, d)

        def _layer(x, wqkv, qs, ksc, wo, lg, lb, w1, b1, w2, b2):
            b, n, _ = x.shape
            h = shift_token(x)
            qkv = h @ wqkv
            q, k, v = jnp.split(qkv, 3, axis=-1)
            to_heads = lambda t: t.reshape(b, n, HEADS, DIM_HEAD).transpose(0, 2, 1, 3)
            q, k, v = (to_heads(q), to_heads(k), to_heads(v))
            q = l2norm(q) * qs
            k = l2norm(k) * ksc
            q, k = rotary_xpos(q, k)
            o = local_attention(q, k, v)
            o = o.transpose(0, 2, 1, 3).reshape(b, n, INNER)
            x = x + o @ wo
            h = shift_token(x)
            mu = h.mean(-1, keepdims=True)
            var = h.var(-1, keepdims=True)
            h = (h - mu) / jnp.sqrt(var + 1e-05) * lg + lb
            h = h @ w1 + b1
            a, g = jnp.split(h, 2, axis=-1)
            h = a * jax.nn.gelu(g, approximate=False)
            x = x + h @ w2 + b2
            return x
        key = jax.random.key(seed)
        ks = jax.random.split(key, 6)
        return {'x': jax.random.normal(ks[0], (B, N, DIM), jnp.float32), 'wqkv': jax.random.normal(ks[1], (DEPTH, DIM, 3 * INNER), jnp.float32) * 0.02, 'q_scale': jnp.ones((DEPTH, DIM_HEAD), jnp.float32), 'k_scale': jnp.ones((DEPTH, DIM_HEAD), jnp.float32), 'wo': jax.random.normal(ks[2], (DEPTH, INNER, DIM), jnp.float32) * 0.02, 'ln_g': jnp.ones((DEPTH, DIM), jnp.float32), 'ln_b': jnp.zeros((DEPTH, DIM), jnp.float32), 'w1': jax.random.normal(ks[3], (DEPTH, DIM, 2 * HID), jnp.float32) * 0.02, 'b1': jnp.zeros((DEPTH, 2 * HID), jnp.float32), 'w2': jax.random.normal(ks[4], (DEPTH, HID, DIM), jnp.float32) * 0.02, 'b2': jnp.zeros((DEPTH, DIM), jnp.float32)}
    _L0_ffn_in = _L0_ffn_setup()

    def _L1_attn_setup():
        import jax, jax.numpy as jnp
        import numpy as np
        B, S, D, H = (2, 256, 128, 16)
        HD = D // H
        key = jax.random.key(seed)
        ks = jax.random.split(key, 9)
        s = 1.0 / np.sqrt(D)
        return {'x': jax.random.normal(ks[0], (B, S, D), dtype=jnp.float32), 'Wk': jax.random.uniform(ks[1], (D, D), jnp.float32, -s, s), 'bk': jax.random.uniform(ks[2], (D,), jnp.float32, -s, s), 'Wq': jax.random.uniform(ks[3], (D, D), jnp.float32, -s, s), 'bq': jax.random.uniform(ks[4], (D,), jnp.float32, -s, s), 'Wv': jax.random.uniform(ks[5], (D, D), jnp.float32, -s, s), 'bv': jax.random.uniform(ks[6], (D,), jnp.float32, -s, s), 'Wo': jax.random.uniform(ks[7], (D, D), jnp.float32, -s, s), 'bo': jax.random.uniform(ks[8], (D,), jnp.float32, -s, s)}
    _L1_attn_in = _L1_attn_setup()

    def _L1_ffn_setup():
        import jax, jax.numpy as jnp
        import numpy as np
        B, S, D = (2, 256, 128)
        H = 256
        E = 8
        K = 2
        HS = 256 * 1
        SCALE = 1.0 / float(np.sqrt(D))
        key = jax.random.key(seed)
        ks = jax.random.split(key, 9)
        init = 0.02
        return {'x': jax.random.normal(ks[0], (B, S, D), dtype=jnp.float32), 'Wr': jax.random.normal(ks[1], (D, E), dtype=jnp.float32) * init, 'rb': jnp.zeros((E,), dtype=jnp.float32), 'W1': jax.random.normal(ks[2], (E, D, H), dtype=jnp.float32) * init, 'W2': jax.random.normal(ks[3], (E, H, D), dtype=jnp.float32) * init, 'W3': jax.random.normal(ks[4], (E, D, H), dtype=jnp.float32) * init, 'Ws1': jax.random.normal(ks[5], (D, HS), dtype=jnp.float32) * init, 'Ws2': jax.random.normal(ks[6], (HS, D), dtype=jnp.float32) * init, 'Ws3': jax.random.normal(ks[7], (D, HS), dtype=jnp.float32) * init}
    _L1_ffn_in = _L1_ffn_setup()
    _d = {'L0_attn_x': _L0_attn_in['x'], 'L0_attn_q_w': _L0_attn_in['q_w'], 'L0_attn_q_b': _L0_attn_in['q_b'], 'L0_attn_k_w': _L0_attn_in['k_w'], 'L0_attn_k_b': _L0_attn_in['k_b'], 'L0_attn_v_w': _L0_attn_in['v_w'], 'L0_attn_v_b': _L0_attn_in['v_b'], 'L0_attn_out_w': _L0_attn_in['out_w'], 'L0_attn_out_b': _L0_attn_in['out_b'], 'L0_attn_proj': _L0_attn_in['proj'], 'L0_attn_gamma': _L0_attn_in['gamma'], 'L0_attn_beta': _L0_attn_in['beta'], 'L0_ffn_wqkv': _L0_ffn_in['wqkv'], 'L0_ffn_q_scale': _L0_ffn_in['q_scale'], 'L0_ffn_k_scale': _L0_ffn_in['k_scale'], 'L0_ffn_wo': _L0_ffn_in['wo'], 'L0_ffn_ln_g': _L0_ffn_in['ln_g'], 'L0_ffn_ln_b': _L0_ffn_in['ln_b'], 'L0_ffn_w1': _L0_ffn_in['w1'], 'L0_ffn_b1': _L0_ffn_in['b1'], 'L0_ffn_w2': _L0_ffn_in['w2'], 'L0_ffn_b2': _L0_ffn_in['b2'], 'L1_attn_Wk': _L1_attn_in['Wk'], 'L1_attn_bk': _L1_attn_in['bk'], 'L1_attn_Wq': _L1_attn_in['Wq'], 'L1_attn_bq': _L1_attn_in['bq'], 'L1_attn_Wv': _L1_attn_in['Wv'], 'L1_attn_bv': _L1_attn_in['bv'], 'L1_attn_Wo': _L1_attn_in['Wo'], 'L1_attn_bo': _L1_attn_in['bo'], 'L1_ffn_Wr': _L1_ffn_in['Wr'], 'L1_ffn_rb': _L1_ffn_in['rb'], 'L1_ffn_W1': _L1_ffn_in['W1'], 'L1_ffn_W2': _L1_ffn_in['W2'], 'L1_ffn_W3': _L1_ffn_in['W3'], 'L1_ffn_Ws1': _L1_ffn_in['Ws1'], 'L1_ffn_Ws2': _L1_ffn_in['Ws2'], 'L1_ffn_Ws3': _L1_ffn_in['Ws3']}
    _x0 = _d['L0_attn_x']
    _d['L0_attn_x'] = jax.random.normal(jax.random.fold_in(jax.random.key(seed), 1), (16, 256, 128), dtype=_x0.dtype)
    del _x0
    return _d

def reference(L0_attn_x, L0_attn_q_w, L0_attn_q_b, L0_attn_k_w, L0_attn_k_b, L0_attn_v_w, L0_attn_v_b, L0_attn_out_w, L0_attn_out_b, L0_attn_proj, L0_attn_gamma, L0_attn_beta, L0_ffn_wqkv, L0_ffn_q_scale, L0_ffn_k_scale, L0_ffn_wo, L0_ffn_ln_g, L0_ffn_ln_b, L0_ffn_w1, L0_ffn_b1, L0_ffn_w2, L0_ffn_b2, L1_attn_Wk, L1_attn_bk, L1_attn_Wq, L1_attn_bq, L1_attn_Wv, L1_attn_bv, L1_attn_Wo, L1_attn_bo, L1_ffn_Wr, L1_ffn_rb, L1_ffn_W1, L1_ffn_W2, L1_ffn_W3, L1_ffn_Ws1, L1_ffn_Ws2, L1_ffn_Ws3):

    def _L0_attn_ref(x, q_w, q_b, k_w, k_b, v_w, v_b, out_w, out_b, proj, gamma, beta):
        import jax, jax.numpy as jnp
        import numpy as np
        B, S, E, H, M = (4, 256, 128, 16, 32)
        D = E // H
        LN_EPS = 1e-06

        def softmax_kernel(x, proj):
            x = x * (1.0 / jnp.sqrt(jnp.asarray(x.shape[-1], x.dtype)))
            mapping = jnp.einsum('bhsd,md->bhsm', x, proj)
            correction = jnp.sum(x * x, axis=-1, keepdims=True) * 0.5
            scaling = 1.0 / jnp.sqrt(jnp.asarray(proj.shape[0], x.dtype))
            return scaling * jnp.exp(mapping - correction)

        def favor_forward(x, q_w, q_b, k_w, k_b, v_w, v_b, out_w, out_b, proj, gamma, beta):
            b, s, e = x.shape
            split = lambda y: y.reshape(b, s, H, D).transpose(0, 2, 1, 3)
            Q = split(x @ q_w + q_b)
            K = split(x @ k_w + k_b)
            V = split(x @ v_w + v_b)
            qp = softmax_kernel(Q, proj).transpose(2, 0, 1, 3)
            kp = softmax_kernel(K, proj).transpose(2, 0, 1, 3)
            vs = V.transpose(2, 0, 1, 3)

            def step(carry, inp):
                ksum, kv = carry
                q, k, v = inp
                ksum = ksum + k
                kv = kv + k[..., :, None] * v[..., None, :]
                num = jnp.einsum('bhmd,bhm->bhd', kv, q)
                den = jnp.einsum('bhm,bhm->bh', q, ksum)
                return ((ksum, kv), (num, den))
            init = (jnp.zeros((b, H, M), x.dtype), jnp.zeros((b, H, M, D), x.dtype))
            _, (num, den) = jax.lax.scan(step, init, (qp, kp, vs))
            attn = num / den[..., None]
            attn = attn.transpose(1, 0, 2, 3).reshape(b, s, e)
            main = attn @ out_w + out_b
            res = main + x
            mu = jnp.mean(res, axis=-1, keepdims=True)
            var = jnp.mean(jnp.square(res - mu), axis=-1, keepdims=True)
            return gamma * (res - mu) * jax.lax.rsqrt(var + LN_EPS) + beta
        return favor_forward(x, q_w, q_b, k_w, k_b, v_w, v_b, out_w, out_b, proj, gamma, beta)

    def _L0_ffn_ref(x, wqkv, q_scale, k_scale, wo, ln_g, ln_b, w1, b1, w2, b2):
        import jax, jax.numpy as jnp
        import numpy as np
        DIM = 128
        DEPTH = 2
        HEADS = 8
        DIM_HEAD = 64
        WINDOW = 64
        INNER = HEADS * DIM_HEAD
        HID = int(DIM * 4 * 2 / 3)
        B, N = (2, 1024)
        QK_SCALE = 8.0

        def shift_token(t):
            t1, t2 = jnp.split(t, 2, axis=-1)
            t2 = jnp.pad(t2, ((0, 0), (1, 0), (0, 0)))[:, :-1]
            return jnp.concatenate([t1, t2], axis=-1)

        def l2norm(t):
            return t / jnp.clip(jnp.linalg.norm(t, axis=-1, keepdims=True), 1e-12)

        def rotate_half(x):
            x1, x2 = jnp.split(x, 2, axis=-1)
            return jnp.concatenate([-x2, x1], axis=-1)

        def rotary_xpos(q, k):
            n = q.shape[-2]
            half_idx = jnp.arange(0, DIM_HEAD, 2, dtype=jnp.float32)
            inv_freq = 1.0 / 10000.0 ** (half_idx / DIM_HEAD)
            t = jnp.arange(n, dtype=jnp.float32)
            freqs = t[:, None] * inv_freq[None, :]
            freqs = jnp.concatenate([freqs, freqs], axis=-1)
            base = (half_idx + 0.4 * DIM_HEAD) / (1.4 * DIM_HEAD)
            power = (t - n // 2) / float(WINDOW // 2)
            scale = base[None, :] ** power[:, None]
            scale = jnp.concatenate([scale, scale], axis=-1)
            cos, sin = (jnp.cos(freqs), jnp.sin(freqs))
            q = q * cos * scale + rotate_half(q) * sin * scale
            k = k * cos / scale + rotate_half(k) * sin / scale
            return (q, k)

        def local_attention(q, k, v):
            b, h, n, d = q.shape
            w = n // WINDOW
            bq = q.reshape(b, h, w, WINDOW, d) * QK_SCALE
            bk = k.reshape(b, h, w, WINDOW, d)
            bv = v.reshape(b, h, w, WINDOW, d)

            def look_around(t):
                p = jnp.pad(t, ((0, 0), (0, 0), (1, 0), (0, 0), (0, 0)))
                return jnp.concatenate([p[:, :, :w], p[:, :, 1:]], axis=3)
            bk, bv = (look_around(bk), look_around(bv))
            bt = jnp.arange(n).reshape(w, WINDOW)
            btp = jnp.pad(bt, ((1, 0), (0, 0)), constant_values=-1)
            btk = jnp.concatenate([btp[:w], btp[1:]], axis=1)
            sim = jnp.einsum('bhwid,bhwjd->bhwij', bq, bk)
            i = bt[:, :, None]
            j = btk[:, None, :]
            mask = (i < j) | (i > j + WINDOW) | (j == -1)
            sim = jnp.where(mask, -jnp.finfo(sim.dtype).max, sim)
            attn = jax.nn.softmax(sim, axis=-1)
            out = jnp.einsum('bhwij,bhwjd->bhwid', attn, bv)
            return out.reshape(b, h, n, d)

        def _layer(x, wqkv, qs, ksc, wo, lg, lb, w1, b1, w2, b2):
            b, n, _ = x.shape
            h = shift_token(x)
            qkv = h @ wqkv
            q, k, v = jnp.split(qkv, 3, axis=-1)
            to_heads = lambda t: t.reshape(b, n, HEADS, DIM_HEAD).transpose(0, 2, 1, 3)
            q, k, v = (to_heads(q), to_heads(k), to_heads(v))
            q = l2norm(q) * qs
            k = l2norm(k) * ksc
            q, k = rotary_xpos(q, k)
            o = local_attention(q, k, v)
            o = o.transpose(0, 2, 1, 3).reshape(b, n, INNER)
            x = x + o @ wo
            h = shift_token(x)
            mu = h.mean(-1, keepdims=True)
            var = h.var(-1, keepdims=True)
            h = (h - mu) / jnp.sqrt(var + 1e-05) * lg + lb
            h = h @ w1 + b1
            a, g = jnp.split(h, 2, axis=-1)
            h = a * jax.nn.gelu(g, approximate=False)
            x = x + h @ w2 + b2
            return x
        for l in range(DEPTH):
            x = _layer(x, wqkv[l], q_scale[l], k_scale[l], wo[l], ln_g[l], ln_b[l], w1[l], b1[l], w2[l], b2[l])
        return x

    def _L1_attn_ref(x, Wk, bk, Wq, bq, Wv, bv, Wo, bo):
        import jax, jax.numpy as jnp
        import numpy as np
        B, S, D, H = (2, 256, 128, 16)
        HD = D // H
        b, s, _ = x.shape

        def proj(W, bias):
            return (x @ W.T + bias).reshape(b, s, H, HD).transpose(0, 2, 1, 3)
        k = proj(Wk, bk)
        q = proj(Wq, bq)
        v = proj(Wv, bv)
        att = jnp.einsum('bhqd,bhkd->bhqk', q, k) / jnp.sqrt(jnp.float32(HD))
        att = jax.nn.softmax(att, axis=-1)
        out = jnp.einsum('bhqk,bhkd->bhqd', att, v)
        out = out.transpose(0, 2, 1, 3).reshape(b, s, D)
        return out @ Wo.T + bo

    def _L1_ffn_ref(x, Wr, rb, W1, W2, W3, Ws1, Ws2, Ws3):
        import jax, jax.numpy as jnp
        import numpy as np
        B, S, D = (2, 256, 128)
        H = 256
        E = 8
        K = 2
        HS = 256 * 1
        SCALE = 1.0 / float(np.sqrt(D))
        logits = jnp.einsum('bsd,de->bse', x, Wr) * SCALE
        _, idx = jax.lax.top_k(logits + rb, K)
        gathered = jnp.take_along_axis(logits, idx, axis=-1)
        w = jax.nn.softmax(gathered, axis=-1)
        w_full = jnp.sum(jax.nn.one_hot(idx, E, dtype=x.dtype) * w[..., None], axis=-2)
        h = jnp.einsum('bsd,edh->bseh', x, W1) * jax.nn.silu(jnp.einsum('bsd,edh->bseh', x, W3))
        expert_out = jnp.einsum('bseh,ehd->bsed', h, W2)
        out = jnp.einsum('bsed,bse->bsd', expert_out, w_full)
        hs = jnp.einsum('bsd,dh->bsh', x, Ws1) * jax.nn.silu(jnp.einsum('bsd,dh->bsh', x, Ws3))
        out = out + jnp.einsum('bsh,hd->bsd', hs, Ws2)
        return out
    x = L0_attn_x
    xn = _layernorm(x, axis=-1)
    x = x + _L0_attn_ref(xn, L0_attn_q_w, L0_attn_q_b, L0_attn_k_w, L0_attn_k_b, L0_attn_v_w, L0_attn_v_b, L0_attn_out_w, L0_attn_out_b, L0_attn_proj, L0_attn_gamma, L0_attn_beta) + _L0_ffn_ref(xn, L0_ffn_wqkv, L0_ffn_q_scale, L0_ffn_k_scale, L0_ffn_wo, L0_ffn_ln_g, L0_ffn_ln_b, L0_ffn_w1, L0_ffn_b1, L0_ffn_w2, L0_ffn_b2)
    xn = _layernorm(x, axis=-1)
    x = x + _L1_attn_ref(xn, L1_attn_Wk, L1_attn_bk, L1_attn_Wq, L1_attn_bq, L1_attn_Wv, L1_attn_bv, L1_attn_Wo, L1_attn_bo) + _L1_ffn_ref(xn, L1_ffn_Wr, L1_ffn_rb, L1_ffn_W1, L1_ffn_W2, L1_ffn_W3, L1_ffn_Ws1, L1_ffn_Ws2, L1_ffn_Ws3)
    return x

_drawn_inputs = setup_inputs


def setup_inputs(seed=0):
    import zlib

    import numpy as np

    out = dict(_drawn_inputs(seed))
    spreads = {'L0_attn_q_b': (0.0, 0.8),
     'L0_attn_k_b': (0.0, 0.8),
     'L0_attn_v_b': (0.0, 0.1),
     'L0_attn_out_b': (0.0, 0.1),
     'L0_attn_gamma': (1.0, 0.2),
     'L0_attn_beta': (0.0, 0.274),
     'L0_ffn_q_scale': (1.0, 0.6),
     'L0_ffn_k_scale': (1.0, 0.6),
     'L0_ffn_ln_g': (1.0, 0.6),
     'L0_ffn_ln_b': (0.0, 0.8),
     'L0_ffn_b1': (0.0, 0.8),
     'L0_ffn_b2': (0.0, 0.1),
     'L1_ffn_rb': (0.0, 0.8)}
    factors = {'L0_ffn_wqkv': 5.125,
     'L0_ffn_wo': 5.13,
     'L0_ffn_w1': 8.0,
     'L0_ffn_w2': 8.0,
     'L1_attn_Wk': 8.0,
     'L1_attn_bk': 8.0,
     'L1_attn_Wq': 8.0,
     'L1_attn_bq': 8.0,
     'L1_attn_Wv': 5.194,
     'L1_attn_bv': 5.592,
     'L1_attn_Wo': 4.116,
     'L1_attn_bo': 3.215,
     'L1_ffn_Wr': 8.0,
     'L1_ffn_W1': 8.0,
     'L1_ffn_W2': 8.0,
     'L1_ffn_W3': 8.0,
     'L1_ffn_Ws1': 8.0,
     'L1_ffn_Ws2': 8.0,
     'L1_ffn_Ws3': 8.0}
    for name, (base, spread) in spreads.items():
        noise = np.random.default_rng([zlib.crc32(name.encode()), seed]).standard_normal(out[name].shape)
        drawn = base * np.exp(spread * noise) if base else spread * noise
        out[name] = jnp.asarray(drawn.astype(out[name].dtype))
    for name, factor in factors.items():
        out[name] = (out[name] * factor).astype(out[name].dtype)
    return out
```

```python
from contextlib import ExitStack

import numpy as np

import concourse.bass as bass
from concourse import mybir

ALU = mybir.AluOpType
ACT = mybir.ActivationFunctionType
AX = mybir.AxisListType
F32 = mybir.dt.float32
BF16 = mybir.dt.bfloat16
I32 = mybir.dt.int32

P = 128
BATCHES, SEQ, D = 16, 256, 128
G = 2
T = G * SEQ
TT = T // P
TURNS = BATCHES // G

FH, FD, FM = 16, 8, 32
LH, LD, WIN, DEPTH = 8, 64, 64, 2
INNER = LH * LD
HID = int(D * 4 * 2 / 3)
HC = [(0, 128), (128, 128), (256, HID - 256)]
AH, AD = 16, 8
EX, EH = 8, 256
NEG = -1e30
LSPAN = 192 + 128

COUNTS = {
    "xnT_ps": 1, "favor_qk_ps": 2, "favor_map_ps": 8, "favor_v_ps": 1, "favor_score_ps": 32,
    "favor_pv": 32, "favor_aT_ps": 1, "favor_out_ps": 1,
    "loc_raw_ps": 16, "loc_sw_ps": 16, "loc_sum_ps": 2, "loc_rT_ps": 2, "loc_rb_ps": 16, "loc_v_ps": 8,
    "loc_max_ps": 16, "loc_nmT_ps": 2, "loc_sT_ps": 32, "loc_pv": 32, "loc_oT_ps": 8, "loc_wo_ps": 2,
    "glu_mean_ps": 2, "glu_var_ps": 2, "glu_rb_ps": 2, "glu_a_ps": 6, "glu_g_ps": 6, "glu_out_ps": 2,
    "yT_ps": 1,
    "xn2T_ps": 1, "att_qk_ps": 8, "att_v_ps": 1, "att_max_ps": 32, "att_nmT_ps": 1, "att_sT_ps": 32,
    "att_pv": 32, "att_oT_ps": 1, "route_ps": 1, "moe_g_ps": 18, "moe_u_ps": 18, "moe_out_ps": 8,
    "final_ps": 1,
    "xnT": 1, "hT": 4, "favor_qk": 2, "favor_sq": 2, "favor_phi": 8, "favor_aT": 1,
    "loc_sq": 16, "loc_rT": 2, "loc_v": 8, "loc_nmT": 2, "loc_p": 32, "loc_oT": 8,
    "glu_h": 4, "glu_sq": 2, "glu_gate": 6,
    "xn2T": 1, "att_qk": 8, "att_nmT": 1, "att_p": 32, "att_oT": 1, "route_exp": 1, "moe_silu": 18,
    "xn": 1, "favor_v": 1, "favor_p": 32, "favor_att": 2, "favor_res": 1, "favor_norm": 1,
    "loc_c": 16, "loc_s": 16, "loc_sum": 2, "loc_rs": 2, "loc_qk": 16, "loc_mx": 16, "loc_nm": 2,
    "loc_o": 8, "loc_x": 2,
    "glu_cen": 2, "glu_var": 2, "glu_rs": 2, "glu_hn": 2, "glu_hid": 6, "glu_x": 2,
    "x1": 1, "xn2": 1, "att_v": 1, "att_mx": 32, "att_nm": 1, "att_o": 2, "route_l": 1, "route_w": 1,
    "moe_h": 18, "moe_acc": 8, "result": 1,
    "vec_step": 178,
    "x_kept": 1, "loc_rot": 16, "favor_done": 1, "pool_step": 2,
}


def consts():
    f, b = np.float32, mybir.dt.np(BF16)
    p = np.arange(P)
    c = {}
    c["ident"] = np.eye(P, dtype=f)
    c["ident4"] = np.tile(np.eye(P), (1, 4)).astype(b)
    c["block8"] = ((p[:, None] % 32) // FD == p[None, :] // FM).astype(f)
    tri = (p[:, None] <= p[None, :]).astype(f)
    c["causal"] = np.concatenate([tri, np.ones((P, P), f), tri], 1)
    q, k = p[:, None], p[None, :]
    ok0 = (k <= q) & (k >= q - WIN)
    r = q % WIN
    ok1 = (k >= r) & (k <= r + WIN)
    c["winmask"] = np.stack([np.where(o, 0, NEG).T for o in (ok0, ok1)], 1).astype(b)
    kk, qq = p[:, None], np.arange(192)[None, :]
    band = np.where((qq >= kk) & (qq <= kk + WIN), 0, NEG)
    c["bandmask"] = np.concatenate([band, band[:, :P]], 1).astype(b)
    s8 = np.zeros((P, LH, P))
    for h in range(LH):
        s8[[LD * (h % 2) + h, LD * (h % 2) + LH + h], h] = 1
    c["sel8"] = s8.astype(b)
    s16 = np.zeros((P, AH, P))
    for h in range(AH):
        s16[[32 * (h % 4) + h, 32 * (h % 4) + AH + h], h] = 1
    c["sel16"] = s16.astype(b)
    c["half"] = (p[:, None] // LD == np.arange(2)[None, :]).astype(f)
    hs = np.zeros((16, 8, P), f)
    for i in range(8):
        hs[2 * i, i, :LD] = 1
        hs[2 * i + 1, i, LD:] = 1
    c["headrow"] = hs
    c["mean"] = np.full((P, P), 1.0 / D, f)
    c["rank"] = np.tile(EX - np.arange(EX, dtype=f), (P, 1))
    half = np.arange(0, LD, 2, dtype=f)
    inv = (f(1) / f(10000.0) ** (half / f(LD))).astype(f)
    t = np.arange(SEQ, dtype=f)
    fr = np.concatenate([t[:, None] * inv[None]] * 2, 1)
    base = (half + f(0.4 * LD)) / f(1.4 * LD)
    sc = base[None] ** ((t - SEQ // 2) / f(WIN // 2))[:, None]
    sc = np.concatenate([sc] * 2, 1).astype(f)
    sign = np.where(np.arange(LD) < LD // 2, -1, 1).astype(f)
    tabs = [np.cos(fr) * sc * f(8), np.sin(fr) * sc * sign * f(8), np.cos(fr) / sc, np.sin(fr) / sc * sign]
    c["rotary"] = np.stack([np.tile(x.T, (2, 1)) for x in tabs], 1).astype(f)
    return c


def build(nc, w, x, out):
    with ExitStack() as ctx:
        def sb(name, shape, dt=F32):
            return ctx.enter_context(nc.sbuf_tensor(name, shape, dt))

        bank = [ctx.enter_context(nc.psum_tensor(f"bank{i}", [P, 512], F32)) for i in range(8)]
        sem = {n: ctx.enter_context(nc.semaphore(n)) for n in COUNTS}
        loaded = ctx.enter_context(nc.semaphore("weights_loaded"))
        prep = ctx.enter_context(nc.semaphore("vector_prepared"))
        prep_ps = ctx.enter_context(nc.semaphore("bias_products"))
        started = ctx.enter_context(nc.semaphore("pool_prepared"))
        x_in_sem = ctx.enter_context(nc.semaphore("x_loaded"))
        stored = ctx.enter_context(nc.semaphore("stored"))

        W = {}
        for n, ap in w.items():
            W[n] = sb("w_" + n, list(ap.shape), ap.dtype)
        fbias = sb("fbias", [P, 2])
        projblk = sb("projblk", [P, P])
        sqblk = sb("sqblk", [P, P])
        rot = sb("rot", [P, DEPTH, 4, SEQ])
        wsw = sb("wsw", [P, DEPTH, 2 * INNER])
        w1s = W["w1"]
        b1s = sb("b1s", [P, DEPTH * 6])
        wpad = sb("wpad", [P, 2, 4, 4, 32])
        apb = sb("apb", [P, 8])
        phibias = sb("phibias", [P, 1])

        x_in = sb("x_in", [P, TT, D])
        x1 = sb("x1", [P, TT, D])
        st = sb("st", [P, TT, 6])
        mv = sb("mv", [P, TT, 2])
        xn = sb("xn", [P, TT, D])
        xnT = sb("xnT", [P, T])
        hT = sb("hT", [P, G, SEQ + 1])
        rs = sb("rs", [P, 64])
        ra = sb("ra", [P, 64])
        rt = sb("rt", [P, 64])
        fqs = sb("fqs", [P, 4, T])
        fqk, fsq = fqs[:, 0:2, :], fqs[:, 2:4, :]
        phi = sb("phi", [P, 8, T])
        fv = sb("fv", [P, TT, FH, FD + 1])
        fp = sb("fp", [P, 4, 384])
        rec = sb("rec", [P, G, 2, 16])
        ftm = sb("ftm", [P, TT, D])
        ftT = sb("ftT", [P, T])
        res = sb("res", [P, TT, D])
        lsq = sb("lsq", [P, 2, T])
        lc = sb("lc", [P, 8, T])
        ls = sb("ls", [P, 2, T])
        lsum = sb("lsum", [P, TT * 16])
        lrT = sb("lrT", [16, T])
        lv = sb("lv", [P, TT, LH, LD + 1])
        lmx = sb("lmx", [P, TT, LH])
        lnm = sb("lnm", [P, TT, 2, LD], BF16)
        lnmT = sb("lnmT", [P, T], BF16)
        lp = fp[:].rearrange("p a b -> p (a b)")[:, 0:4 * LSPAN].rearrange("p (a b) -> p a b", a=4)
        loT = phi[:, 0:4, :]
        lo = phi[:, 4:8, :]
        xB = sb("xB", [P, T])
        cen = sb("cen", [P, T])
        csq = lsq[:, 0, :]
        var = sb("var", [P, TT])
        gate = ls
        hid = fqs[:, 0:3, :]
        xn2T = sb("xn2T", [P, T])
        aqk = phi
        av = fv
        amx = sb("amx", [P, TT, AH])
        anm = sb("anm", [P, TT, 4, 2, AH], BF16)
        anmT = sb("anmT", [P, T], BF16)
        apr = fp[:].rearrange("p a b -> p (a b)").rearrange("p (a b) -> p a b", a=3)
        route = sb("route", [P, 10, TT * EX])
        rsm = sb("rsm", [P, 8, TT])
        silu = lc[:, 4:6, :]
        mh = lc[:, 0:4, :]
        moe = sb("moe", [P, TT, D])

        block = ctx.enter_context(nc.Block())

        RINGS = {"short": ([], 0, 6), "long": ([], 6, 2)}
        LONG = ("favor_pv", "loc_pv", "att_pv", "loc_sum")

        def job(name, k, freed_by, count):
            RINGS["long" if name in LONG else "short"][0].append((name, k, freed_by, count))

        job("xnT", 0, "hT", 2)
        for i in range(2):
            job("favor_qk", i, "favor_qk", i + 1)
        job("favor_v", 0, "favor_v", 1)
        for i in range(8):
            job("favor_map", i, "favor_phi", i + 1)
        for b in range(G):
            job("favor_pv", b, "favor_att", b + 1)
            for h in range(FH):
                job("favor_score", b * FH + h, "favor_p", b * FH + h + 1)
        job("favor_aT", 0, "favor_aT", 1)
        job("favor_out", 0, "favor_res", 1)
        for l in range(DEPTH):
            job("loc_sum", l, "loc_sum", l + 1)
            for c in range(8):
                job("loc_raw", 8 * l + c, "loc_sq", 8 * l + c + 1)
                job("loc_sw", 8 * l + c, "loc_s", 8 * l + c + 1)
            for j in range(TT):
                job("loc_v", TT * l + j, "loc_v", TT * l + j + 1)
            job("loc_rT", l, "loc_rT", l + 1)
            for c in range(8):
                job("loc_rb", 8 * l + c, "loc_qk", 8 * l + c + 1)
            for j in range(8):
                job("loc_max", 8 * l + j, "loc_mx", 8 * l + j + 1)
            job("loc_nmT", l, "loc_nmT", l + 1)
            for b in range(G):
                for hg in range(2):
                    job("loc_pv", ((l * G + b) * 2 + hg) * 2, "loc_o", 4 * l + 2 * b + hg + 1)
                    job("loc_pv", ((l * G + b) * 2 + hg) * 2 + 1, "loc_o", 4 * l + 2 * b + hg + 1)
                    for h in range(4):
                        n = (l * G + b) * 8 + hg * 4 + h
                        job("loc_sT", n, "loc_p", n + 1)
            for c in range(4):
                job("loc_oT", 4 * l + c, "loc_oT", 4 * l + c + 1)
            job("loc_wo", l, "loc_x", l + 1)
            job("glu_mean", l, "glu_cen", l + 1)
            job("glu_var", l, "glu_var", l + 1)
            job("glu_rb", l, "glu_hn", l + 1)
            for c in range(3):
                job("glu_g", 3 * l + c, "glu_gate", 3 * l + c + 1)
                job("glu_a", 3 * l + c, "glu_hid", 3 * l + c + 1)
            job("glu_out", l, "glu_x", l + 1)
        job("yT", 0, "x1", 1)
        job("xn2T", 0, "xn2T", 1)
        for i in range(8):
            job("att_qk", i, "att_qk", i + 1)
        job("att_v", 0, "att_v", 1)
        job("route", 0, "route_l", 1)
        for i in range(32):
            job("att_max", i, "att_mx", i + 1)
        job("att_nmT", 0, "att_nmT", 1)
        for b in range(G):
            job("att_pv", b, "att_o", b + 1)
            for h in range(AH):
                job("att_sT", b * AH + h, "att_p", b * AH + h + 1)
        job("att_oT", 0, "att_oT", 1)
        for e in range(EX + 1):
            for j in range(2):
                job("moe_g", 2 * e + j, "moe_silu", 2 * e + j + 1)
                job("moe_u", 2 * e + j, "moe_h", 2 * e + j + 1)
            if e < EX:
                job("moe_out", e, "moe_acc", e + 1)
            else:
                job("final", 0, "result", 1)
        AT = {(n, k): (i, ring) for ring in RINGS.values() for i, (n, k, _, _) in enumerate(ring[0])}

        def bank_of(name, k=0):
            i, (_, first, size) = AT[name, k]
            return bank[first + i % size]

        def counters(eng, it):
            target = eng.alloc_register("target")

            def value(name, count):
                eng.reg_mul(target, it, COUNTS[name])
                eng.reg_add(target, target, count)
                return target

            def now(name, count):
                return value(name, COUNTS[name] + count)

            def prior(name, count=None):
                return value(name, COUNTS[name] if count is None else count)

            def freed(name, k=0):
                i, (jobs, first, size) = AT[name, k]
                if i >= size:
                    _, _, by, count = jobs[i - size]
                    return sem[by], now(by, count)
                _, _, by, count = jobs[max(j for j in range(len(jobs)) if j % size == i)]
                return sem[by], prior(by, count)

            return now, prior, freed

        @block.sync
        def _(sp):
            for n in COUNTS:
                sp.sem_inc(sem[n], COUNTS[n])
            sp.sem_inc(stored, 16)
            for n, ap in w.items():
                sp.dma_start(W[n][:], ap).then_inc(loaded, 16)
            with sp.Fori(0, TURNS) as it:
                now, prior, freed = counters(sp, it)
                src = x[it]
                sp.wait_ge(sem["x_kept"], prior("x_kept"))
                sp.wait_ge(sem["xn"], prior("xn"))
                sp.dma_start(x_in[:], src).then_inc(x_in_sem, 16)
                dst = out[it]
                sp.wait_ge(sem["result"], now("result", 1))
                sp.dma_start(dst, res[:]).then_inc(stored, 16)
            sp.wait_ge(stored, 16 * (TURNS + 1))

        N_LOADS = len(w)

        @block.gpsimd
        def _(pool):
            pool.wait_ge(loaded, 16 * N_LOADS)
            nc.gpsimd.memset(hT[:], 0.0).then_inc(started, 1)
            nc.gpsimd.memset(fv[:], 1.0).then_inc(started, 1)
            nc.gpsimd.memset(lv[:], 1.0).then_inc(started, 1)
            nc.gpsimd.memset(wpad[:], 0.0).then_inc(started, 1)
            nc.gpsimd.memset(lnm[:], 0.0).then_inc(started, 1)
            nc.gpsimd.memset(phibias[:], -0.5 * float(np.log(FM))).then_inc(started, 1)
            with pool.Fori(0, TURNS) as it:
                now, prior, freed = counters(pool, it)
                def rotate(l):
                    for c in range(8):
                        n = 8 * l + c
                        pool.wait_ge(sem["loc_c"], now("loc_c", n + 1))
                        pool.wait_ge(sem["loc_s"], now("loc_s", n + 1))
                        nc.gpsimd.tensor_tensor(lc[:, c, :], lc[:, c, :], ls[:, c % 2, :],
                                                ALU.add).then_inc(sem["loc_rot"], 1)

                pool.wait_ge(sem["favor_norm"], now("favor_norm", 1))
                rows = lambda i: W["rows"][:, i, :].unsqueeze(1).broadcast_to([P, TT, D])
                nc.gpsimd.tensor_tensor(res[:], res[:], rows(2), ALU.mult).then_inc(sem["pool_step"], 1)
                pool.wait_ge(sem["pool_step"], now("pool_step", 1))
                nc.gpsimd.tensor_tensor(res[:], res[:], rows(3), ALU.add).then_inc(sem["pool_step"], 1)
                pool.wait_ge(sem["pool_step"], now("pool_step", 2))
                pool.wait_ge(sem["x_kept"], now("x_kept", 1))
                nc.gpsimd.tensor_tensor(x1[:], x1[:], res[:], ALU.add).then_inc(sem["favor_done"], 1)
                for l in range(DEPTH):
                    rotate(l)

        @block.tensor
        def _(pe):
            mm = nc.tensor.matmul
            pe.wait_ge(loaded, 16 * N_LOADS)
            pe.wait_ge(prep_ps, 1)
            for l in range(DEPTH):
                for c, (o, m) in enumerate(HC):
                    for g in range(2):
                        last = mm(bank[0][0:m, 6 * l + 2 * c + g:6 * l + 2 * c + g + 1],
                                  W["w1"][:, l, g * HID + o:g * HID + o + m], W["cols"][:, 14 + 1 + l:16 + l],
                                  start=True, stop=True)
            last.then_inc(prep_ps, 1)
            pe.wait_ge(prep, 16)
            pe.wait_ge(started, 6)
            I = W["ident"]
            with pe.Fori(0, TURNS) as it:
                now, prior, freed = counters(pe, it)


                def transpose4(o, src, ready_name, name):
                    for j in range(TT):
                        last = nc.tensor.transpose(o[:, j * P:(j + 1) * P], src[:, j, :], I[:])
                    last.then_inc(sem[name], 1)

                pe.wait_ge(*freed("xnT"))
                o = bank_of("xnT")
                pe.wait_ge(sem["xn"], now("xn", 1))
                transpose4(o, xn, None, "xnT_ps")
                pe.wait_ge(sem["xnT"], now("xnT", 1))
                for i in range(2):
                    pe.wait_ge(*freed("favor_qk", i))
                    o = bank_of("favor_qk", i)
                    mm(o[:], W["fw"][:, i, :], xnT[:], start=True, stop=True).then_inc(sem["favor_qk_ps"], 1)
                pe.wait_ge(*freed("favor_v"))
                o = bank_of("favor_v")
                for j in range(TT):
                    last = mm(o[:, j * P:(j + 1) * P], xnT[:, j * P:(j + 1) * P], W["fw"][:, 2, :],
                              start=True, stop=True)
                last.then_inc(sem["favor_v_ps"], 1)
                for i in range(8):
                    w_, c = divmod(i, 4)
                    r = slice(32 * c, 32 * c + 32)
                    pe.wait_ge(*freed("favor_map", i))
                    o = bank_of("favor_map", i)
                    if c == 0:
                        pe.wait_ge(sem["favor_qk"], now("favor_qk", w_ + 1))
                        pe.wait_ge(sem["favor_sq"], now("favor_sq", w_ + 1))
                    mm(o[:], projblk[r, :], fqk[r, w_, :], start=True, stop=False)
                    mm(o[:], sqblk[r, :], fsq[r, w_, :], start=False, stop=True).then_inc(sem["favor_map_ps"], 1)

                def favor_score(n):
                    b, h = divmod(n, FH)
                    c, r = h // 4, slice(32 * (h % 4), 32 * (h % 4) + 32)
                    pe.wait_ge(*freed("favor_score", n))
                    o = bank_of("favor_score", n)
                    if n == 0:
                        pe.wait_ge(sem["favor_phi"], now("favor_phi", 8))
                    t = b * SEQ
                    mm(o[:, 0:256], phi[r, 4 + c, t:t + P], phi[r, c, t:t + SEQ], start=True, stop=True)
                    mm(o[:, 256:384], phi[r, 4 + c, t + P:t + SEQ], phi[r, c, t + P:t + SEQ],
                            start=True, stop=True).then_inc(sem["favor_score_ps"], 1)

                def favor_pv(n):
                    b, h = divmod(n, FH)
                    if h == 0:
                        pe.wait_ge(*freed("favor_pv", b))
                        pe.wait_ge(sem["favor_v"], now("favor_v", 1))
                    o = bank_of("favor_pv", b)[:, 0:288].rearrange("p (t h d) -> p t h d", t=2, h=FH)
                    p = fp[:, n % 4, :]
                    pe.wait_ge(sem["favor_p"], now("favor_p", n + 1))
                    mm(o[:, 0, h, :], p[:, 0:P], fv[:, 2 * b, h, :], start=True, stop=True)
                    mm(o[:, 1, h, :], p[:, P:2 * P], fv[:, 2 * b, h, :], start=True, stop=False)
                    mm(o[:, 1, h, :], p[:, 2 * P:3 * P], fv[:, 2 * b + 1, h, :], start=False, stop=True).then_inc(sem["favor_pv"], 1)

                for n in range(G * FH + 2):
                    if n < G * FH:
                        favor_score(n)
                    if n >= 2:
                        favor_pv(n - 2)
                pe.wait_ge(*freed("favor_aT"))
                o = bank_of("favor_aT")
                pe.wait_ge(sem["favor_att"], now("favor_att", 2))
                transpose4(o, ftm, None, "favor_aT_ps")
                pe.wait_ge(*freed("favor_out"))
                o = bank_of("favor_out")
                pe.wait_ge(sem["favor_aT"], now("favor_aT", 1))
                for j in range(TT):
                    last = mm(o[:, j * P:(j + 1) * P], ftT[:, j * P:(j + 1) * P], W["fw"][:, 3, :],
                              start=True, stop=True)
                last.then_inc(sem["favor_out_ps"], 1)

                for l in range(DEPTH):
                    h = hT[:, :, 0:SEQ]
                    pe.wait_ge(sem["hT"], now("hT", 2 * (l + 1)))
                    pe.wait_ge(*freed("loc_sum", l))
                    so = bank_of("loc_sum", l)

                    def sums(c):
                        pe.wait_ge(sem["loc_sq"], now("loc_sq", 8 * l + c + 1))
                        for j in range(TT):
                            last = mm(so[:, j * 16 + 2 * c:j * 16 + 2 * c + 2], lsq[:, c % 2, j * P:(j + 1) * P],
                                      W["half"][:], start=True, stop=True)
                        last.then_inc(sem["loc_sum_cols"], 1)

                    for c in range(8):
                        pe.wait_ge(*freed("loc_raw", 8 * l + c))
                        o = bank_of("loc_raw", 8 * l + c)
                        mm(o[:], W["wqkv"][:, l, c * P:(c + 1) * P], h, start=True, stop=True).then_inc(sem["loc_raw_ps"], 1)
                        pe.wait_ge(*freed("loc_sw", 8 * l + c))
                        o = bank_of("loc_sw", 8 * l + c)
                        mm(o[:], wsw[:, l, c * P:(c + 1) * P], h, start=True, stop=True).then_inc(sem["loc_sw_ps"], 1)
                        if c >= 1:
                            sums(c - 1)
                    sums(7)
                    for j in range(TT):
                        pe.wait_ge(*freed("loc_v", TT * l + j))
                        o = bank_of("loc_v", TT * l + j)
                        b, t = divmod(j, 2)
                        mm(o[:], hT[:, b, t * P:(t + 1) * P], W["wqkv"][:, l, 2 * INNER:3 * INNER],
                                start=True, stop=True).then_inc(sem["loc_v_ps"], 1)
                    pe.wait_ge(*freed("loc_rT", l))
                    o = bank_of("loc_rT", l)
                    pe.wait_ge(sem["loc_rs"], now("loc_rs", l + 1))
                    for j in range(TT):
                        last = nc.tensor.transpose(o[0:16, j * P:(j + 1) * P], rs[:, j * 16:(j + 1) * 16], I[:])
                    last.then_inc(sem["loc_rT_ps"], 1)
                    pe.wait_ge(sem["loc_rT"], now("loc_rT", l + 1))
                    for c in range(8):
                        pe.wait_ge(*freed("loc_rb", 8 * l + c))
                        o = bank_of("loc_rb", 8 * l + c)
                        mm(o[:], W["headrow"][:, c, :], lrT[:], start=True, stop=True).then_inc(sem["loc_rb_ps"], 1)
                    pe.wait_ge(sem["loc_qk"], now("loc_qk", 8 * l + 8))
                    for n in range(8):
                        b, t, hg = n // 4, (n // 2) % 2, n % 2
                        pe.wait_ge(*freed("loc_max", 8 * l + n))
                        o = bank_of("loc_max", 8 * l + n)
                        mm(o[:], W["winmask"][:, t, :], W["ident4"][:], start=True, stop=False,
                           skip_group_check=True)
                        for i in range(4):
                            r, c = slice(64 * hg, 64 * hg + 64), i
                            q0 = b * SEQ + t * P
                            oo = o[:, i * P:(i + 1) * P]
                            if t == 0:
                                last = mm(oo, lc[r, c, q0:q0 + P], lc[r, 4 + c, q0:q0 + P],
                                          start=False, stop=True, skip_group_check=True)
                            else:
                                for u in range(2):
                                    k0 = b * SEQ + (u + 1) * WIN
                                    last = mm(oo[u * 64:u * 64 + 64, :],
                                              lc[r, c, q0 + u * 64:q0 + u * 64 + 64], lc[r, 4 + c, k0:k0 + P],
                                              start=False, stop=True, skip_group_check=True)
                        last.then_inc(sem["loc_max_ps"], 1)
                    pe.wait_ge(*freed("loc_nmT", l))
                    o = bank_of("loc_nmT", l).bitcast(BF16)
                    pe.wait_ge(sem["loc_nm"], now("loc_nm", l + 1))
                    for j in range(TT):
                        last = nc.tensor.transpose(o[:, j * P:(j + 1) * P],
                                                   lnm[:, j, :, :].rearrange("p g h -> p (g h)"),
                                                   W["ident4"][:, 0:P])
                    last.then_inc(sem["loc_nmT_ps"], 1)
                    pe.wait_ge(sem["loc_nmT"], now("loc_nmT", l + 1))

                    def loc_sT(n):
                        b, hh = divmod(n, LH)
                        k = l * G * LH + n
                        pe.wait_ge(*freed("loc_sT", k))
                        o = bank_of("loc_sT", k)
                        r, c, t = slice(64 * (hh % 2), 64 * (hh % 2) + 64), hh // 2, b * SEQ
                        mm(o[:, 0:LSPAN], W["ident4"][:, 0:P], W["bandmask"][:], start=True, stop=False,
                           skip_group_check=True)
                        for kt, (c0, q0, nq) in enumerate(((0, 0, 192), (192, P, P))):
                            mm(o[:, c0:c0 + nq], W["sel8"][r, hh, :], lnmT[r, t + q0:t + q0 + nq],
                               start=False, stop=False, skip_group_check=True)
                            last = mm(o[:, c0:c0 + nq], lc[r, 4 + c, t + kt * P:t + kt * P + P],
                                      lc[r, c, t + q0:t + q0 + nq], start=False, stop=True, skip_group_check=True)
                        last.then_inc(sem["loc_sT_ps"], 1)

                    def loc_pv(n):
                        b, hh = divmod(n, LH)
                        k, i = l * G * LH + n, hh % 4
                        j0 = ((l * G + b) * 2 + hh // 4) * 2
                        if i == 0:
                            pe.wait_ge(*freed("loc_pv", j0))
                            pe.wait_ge(*freed("loc_pv", j0 + 1))
                        a, z = [bank_of("loc_pv", j0 + u)[:, i * 65:(i + 1) * 65] for u in range(2)]
                        p = lp[:, k % 4, :]
                        pe.wait_ge(sem["loc_p"], now("loc_p", k + 1))
                        pe.wait_ge(sem["loc_v"], now("loc_v", TT * (l + 1)))
                        v0, v1 = lv[:, 2 * b, hh, :], lv[:, 2 * b + 1, hh, :]
                        mm(a, p[:, 0:P], v0, start=True, stop=True)
                        mm(z, p[:, 192:320], v1, start=True, stop=True)
                        mm(z[0:64, :], p[:, P:192], v0, start=False, stop=True, skip_group_check=True).then_inc(sem["loc_pv"], 1)

                    for n in range(G * LH + 2):
                        if n < G * LH:
                            loc_sT(n)
                        if n >= 2:
                            loc_pv(n - 2)
                    pe.wait_ge(sem["loc_o"], now("loc_o", 4 * (l + 1)))
                    for c in range(4):
                        pe.wait_ge(*freed("loc_oT", 4 * l + c))
                        o = bank_of("loc_oT", 4 * l + c)
                        for j in range(TT):
                            last = nc.tensor.transpose(o[:, j * P:(j + 1) * P], lo[:, j, c * P:(c + 1) * P], I[:])
                        last.then_inc(sem["loc_oT_ps"], 1)
                    pe.wait_ge(*freed("loc_wo", l))
                    o = bank_of("loc_wo", l)
                    for c in range(4):
                        pe.wait_ge(sem["loc_oT"], now("loc_oT", 4 * l + c + 1))
                        last = mm(o[:], W["wo"][:, l, c, :], loT[:, c, :], start=(c == 0), stop=(c == 3))
                    last.then_inc(sem["loc_wo_ps"], 1)
                    pe.wait_ge(*freed("glu_mean", l))
                    o = bank_of("glu_mean", l)
                    pe.wait_ge(sem["glu_h"], now("glu_h", 2 * (l + 1)))
                    mm(o[:], W["mean"][:], h, start=True, stop=True).then_inc(sem["glu_mean_ps"], 1)
                    pe.wait_ge(*freed("glu_var", l))
                    o = bank_of("glu_var", l)
                    pe.wait_ge(sem["glu_sq"], now("glu_sq", l + 1))
                    for j in range(TT):
                        last = mm(o[:, j:j + 1], csq[:, j * P:(j + 1) * P], W["mean"][:, 0:1], start=True, stop=True)
                    last.then_inc(sem["glu_var_ps"], 1)
                    pe.wait_ge(*freed("glu_rb", l))
                    o = bank_of("glu_rb", l)
                    pe.wait_ge(sem["glu_rs"], now("glu_rs", l + 1))
                    for j in range(TT):
                        last = mm(o[:, j * P:(j + 1) * P], rs[:, j:j + 1].broadcast_to([P, P]), I[:],
                                  start=True, stop=True)
                    last.then_inc(sem["glu_rb_ps"], 1)
                    pe.wait_ge(sem["glu_hn"], now("glu_hn", l + 1))
                    for c, (r0, m) in enumerate(HC):
                        pe.wait_ge(*freed("glu_g", 3 * l + c))
                        o = bank_of("glu_g", 3 * l + c)
                        mm(o[0:m, :], w1s[:, l, HID + r0:HID + r0 + m], cen[:], start=True, stop=True).then_inc(sem["glu_g_ps"], 1)
                        pe.wait_ge(*freed("glu_a", 3 * l + c))
                        o = bank_of("glu_a", 3 * l + c)
                        mm(o[0:m, :], w1s[:, l, r0:r0 + m], cen[:], start=True, stop=True).then_inc(sem["glu_a_ps"], 1)
                    pe.wait_ge(*freed("glu_out", l))
                    o = bank_of("glu_out", l)
                    for c, (r0, m) in enumerate(HC):
                        pe.wait_ge(sem["glu_hid"], now("glu_hid", 3 * l + c + 1))
                        last = mm(o[:], W["w2"][0:m, l, c, :], hid[0:m, c, :], start=(c == 0), stop=(c == 2))
                    last.then_inc(sem["glu_out_ps"], 1)
                pe.wait_ge(*freed("yT"))
                o = bank_of("yT")
                pe.wait_ge(sem["glu_x"], now("glu_x", 2))
                for j in range(TT):
                    last = nc.tensor.transpose(o[:, j * P:(j + 1) * P], xB[:, j * P:(j + 1) * P], I[:])
                last.then_inc(sem["yT_ps"], 1)

                pe.wait_ge(*freed("xn2T"))
                o = bank_of("xn2T")
                pe.wait_ge(sem["xn2"], now("xn2", 1))
                transpose4(o, xn, None, "xn2T_ps")
                pe.wait_ge(sem["xn2T"], now("xn2T", 1))
                for i in range(8):
                    pe.wait_ge(*freed("att_qk", i))
                    o = bank_of("att_qk", i)
                    w_ = wpad[:, i // 4, i % 4, :, :].rearrange("p a d -> p (a d)")
                    mm(o[:], w_, xn2T[:], start=True, stop=True).then_inc(sem["att_qk_ps"], 1)
                pe.wait_ge(*freed("att_v"))
                o = bank_of("att_v")
                for j in range(TT):
                    last = mm(o[:, j * P:(j + 1) * P], xn2T[:, j * P:(j + 1) * P], W["aw"][:, 2, :],
                              start=True, stop=True)
                last.then_inc(sem["att_v_ps"], 1)
                pe.wait_ge(*freed("route"))
                o = bank_of("route")
                for j in range(TT):
                    last = mm(o[:, j * EX:(j + 1) * EX], xn2T[:, j * P:(j + 1) * P], W["wr"][:],
                              start=True, stop=True)
                last.then_inc(sem["route_ps"], 1)
                pe.wait_ge(sem["att_qk"], now("att_qk", 8))
                for n in range(G * AH):
                    b, h = divmod(n, AH)
                    r, c, t = slice(32 * (h % 4), 32 * (h % 4) + 32), h // 4, b * SEQ
                    pe.wait_ge(*freed("att_max", n))
                    o = bank_of("att_max", n)
                    for qt in range(2):
                        last = mm(o[:, qt * SEQ:(qt + 1) * SEQ], aqk[r, c, t + qt * P:t + qt * P + P],
                                  aqk[r, 4 + c, t:t + SEQ], start=True, stop=True)
                    last.then_inc(sem["att_max_ps"], 1)
                pe.wait_ge(*freed("att_nmT"))
                o = bank_of("att_nmT").bitcast(BF16)
                pe.wait_ge(sem["att_nm"], now("att_nm", 1))
                for j in range(TT):
                    last = nc.tensor.transpose(o[:, j * P:(j + 1) * P],
                                               anm[:, j, :, :, :].rearrange("p g a h -> p (g a h)"), W["ident4"][:, 0:P])
                last.then_inc(sem["att_nmT_ps"], 1)
                pe.wait_ge(sem["att_nmT"], now("att_nmT", 1))

                def att_sT(n):
                    b, h = divmod(n, AH)
                    r, c, t = slice(32 * (h % 4), 32 * (h % 4) + 32), h // 4, b * SEQ
                    pe.wait_ge(*freed("att_sT", n))
                    o = bank_of("att_sT", n)
                    mm(o[:], W["sel16"][r, h, :], anmT[r, t:t + SEQ].unsqueeze(1).broadcast_to([32, 2, SEQ]),
                       start=True, stop=False, skip_group_check=True)
                    for kt in range(2):
                        last = mm(o[:, kt * SEQ:(kt + 1) * SEQ], aqk[r, 4 + c, t + kt * P:t + kt * P + P],
                                  aqk[r, c, t:t + SEQ], start=False, stop=True, skip_group_check=True)
                    last.then_inc(sem["att_sT_ps"], 1)

                def att_pv(n):
                    b, h = divmod(n, AH)
                    if h == 0:
                        pe.wait_ge(*freed("att_pv", b))
                        pe.wait_ge(sem["att_v"], now("att_v", 1))
                    o = bank_of("att_pv", b)[:, 0:288].rearrange("p (t h d) -> p t h d", t=2, h=AH)
                    pe.wait_ge(sem["att_p"], now("att_p", n + 1))
                    for qt in range(2):
                        for kt in range(2):
                            q0 = kt * SEQ + qt * P
                            last = mm(o[:, qt, h, :], apr[:, n % 3, q0:q0 + P], av[:, 2 * b + kt, h, :],
                                      start=(kt == 0), stop=(kt == 1))
                    last.then_inc(sem["att_pv"], 1)

                for n in range(G * AH + 2):
                    if n < G * AH:
                        att_sT(n)
                    if n >= 2:
                        att_pv(n - 2)
                pe.wait_ge(*freed("att_oT"))
                o = bank_of("att_oT")
                pe.wait_ge(sem["att_o"], now("att_o", 2))
                transpose4(o, ftm, None, "att_oT_ps")

                def expert_out(e):
                    out_bank = ("moe_out", e) if e < EX else ("final", 0)
                    pe.wait_ge(*freed(*out_bank))
                    o = bank_of(*out_bank)
                    pe.wait_ge(sem["moe_h"], now("moe_h", 2 * e + 2))
                    if e == EX:
                        pe.wait_ge(sem["att_oT"], now("att_oT", 1))
                    for j in range(TT):
                        t = slice(j * P, (j + 1) * P)
                        if e == EX:
                            mm(o[:, t], ftT[:, t], W["aw"][:, 3, :], start=True, stop=False)
                        for i in range(2):
                            last = mm(o[:, t], mh[:, (2 * e + i) % 4, t], W["mw2"][:, e, i, :],
                                      start=(e < EX and i == 0), stop=(i == 1))
                    last.then_inc(sem["moe_out_ps" if e < EX else "final_ps"], 1)

                for e in range(EX + 1):
                    for i in range(2):
                        pe.wait_ge(*freed("moe_g", 2 * e + i))
                        o = bank_of("moe_g", 2 * e + i)
                        mm(o[:], W["mw3"][:, e, i * P:(i + 1) * P], xn2T[:], start=True, stop=True).then_inc(sem["moe_g_ps"], 1)
                        pe.wait_ge(*freed("moe_u", 2 * e + i))
                        o = bank_of("moe_u", 2 * e + i)
                        mm(o[:], W["mw1"][:, e, i * P:(i + 1) * P], xn2T[:], start=True, stop=True).then_inc(sem["moe_u_ps"], 1)
                    expert_out(e)

        @block.scalar
        def _(act):
            A = nc.scalar.activation
            act.wait_ge(prep, 16)
            act.wait_ge(started, 6)
            with act.Fori(0, TURNS) as it:
                now, prior, freed = counters(act, it)


                def shifted(src, name, k):
                    A(hT[0:64, :, 0:SEQ], src[0:64, :].rearrange("p (b t) -> p b t", b=G), ACT.Copy).then_inc(sem[name], 1)
                    A(hT[64:P, :, 1:SEQ + 1], src[64:P, :].rearrange("p (b t) -> p b t", b=G), ACT.Copy).then_inc(sem[name], 1)

                act.wait_ge(x_in_sem, it * 16 + 16)
                act.wait_ge(sem["result"], prior("result"))
                A(x1[:], x_in[:], ACT.Copy).then_inc(sem["x_kept"], 1)
                act.wait_ge(sem["xnT_ps"], now("xnT_ps", 1))
                act.wait_ge(sem["glu_x"], prior("glu_x"))
                A(xnT[:], bank_of("xnT")[:], ACT.Copy).then_inc(sem["xnT"], 1)
                shifted(bank_of("xnT"), "hT", 0)
                for i in range(2):
                    act.wait_ge(sem["favor_qk_ps"], now("favor_qk_ps", i + 1))
                    A(fqk[:, i, :], bank_of("favor_qk", i)[:], ACT.Identity, bias=fbias[:, i:i + 1],
                            scale=FD ** -0.5).then_inc(sem["favor_qk"], 1)
                for i in range(2):
                    act.wait_ge(sem["favor_qk"], now("favor_qk", i + 1))
                    A(fsq[:, i, :], fqk[:, i, :], ACT.Square).then_inc(sem["favor_sq"], 1)
                act.wait_ge(sem["att_sT_ps"], prior("att_sT_ps"))
                for i in range(8):
                    act.wait_ge(sem["favor_map_ps"], now("favor_map_ps", i + 1))
                    A(phi[:, i, :], bank_of("favor_map", i)[:], ACT.Exp, bias=phibias[:, 0:1]).then_inc(sem["favor_phi"], 1)
                act.wait_ge(sem["favor_aT_ps"], now("favor_aT_ps", 1))
                act.wait_ge(sem["final_ps"], prior("final_ps"))
                A(ftT[:], bank_of("favor_aT")[:], ACT.Copy).then_inc(sem["favor_aT"], 1)

                for l in range(DEPTH):
                    for c in range(8):
                        n = 8 * l + c
                        act.wait_ge(sem["loc_raw_ps"], now("loc_raw_ps", n + 1))
                        act.wait_ge(sem["loc_c"], now("loc_c", n + 1))
                        if n >= 2:
                            act.wait_ge(sem["loc_sum_cols"], now("loc_sum_cols", n - 1))
                        A(lsq[:, c % 2, :], bank_of("loc_raw", n)[:], ACT.Square).then_inc(sem["loc_sq"], 1)
                    for j in range(TT):
                        n = TT * l + j
                        act.wait_ge(sem["loc_v_ps"], now("loc_v_ps", n + 1))
                        if l:
                            act.wait_ge(sem["loc_pv"], now("loc_pv", 16))
                        A(lv[:, j, :, 0:LD], bank_of("loc_v", n)[:].rearrange("p (h d) -> p h d", h=LH),
                                ACT.Copy).then_inc(sem["loc_v"], 1)
                    act.wait_ge(sem["loc_rT_ps"], now("loc_rT_ps", l + 1))
                    A(lrT[:], bank_of("loc_rT", l)[0:16, :], ACT.Copy).then_inc(sem["loc_rT"], 1)
                    act.wait_ge(sem["loc_nmT_ps"], now("loc_nmT_ps", l + 1))
                    A(lnmT[:], bank_of("loc_nmT", l)[:, 0:256].bitcast(BF16), ACT.Copy).then_inc(sem["loc_nmT"], 1)
                    for k in range(16 * l, 16 * l + 16):
                        act.wait_ge(sem["loc_sT_ps"], now("loc_sT_ps", k + 1))
                        if k >= 4:
                            act.wait_ge(sem["loc_pv"], now("loc_pv", k - 3))
                        A(lp[:, k % 4, :], bank_of("loc_sT", k)[:, 0:LSPAN], ACT.Exp).then_inc(sem["loc_p"], 1)
                    for c in range(4):
                        act.wait_ge(sem["loc_oT_ps"], now("loc_oT_ps", 4 * l + c + 1))
                        if l:
                            act.wait_ge(sem["loc_wo_ps"], now("loc_wo_ps", 1))
                        A(loT[:, c, :], bank_of("loc_oT", 4 * l + c)[:], ACT.Copy).then_inc(sem["loc_oT"], 1)
                    act.wait_ge(sem["loc_x"], now("loc_x", l + 1))
                    shifted(xB, "glu_h", l)
                    act.wait_ge(sem["glu_cen"], now("glu_cen", l + 1))
                    A(csq, cen[:], ACT.Square).then_inc(sem["glu_sq"], 1)
                    for c, (r0, m) in enumerate(HC):
                        n = 3 * l + c
                        act.wait_ge(sem["glu_g_ps"], now("glu_g_ps", n + 1))
                        if n >= 2:
                            act.wait_ge(sem["glu_hid"], now("glu_hid", n - 1))
                        A(gate[0:m, n % 2, :], bank_of("glu_g", n)[0:m, :], ACT.Gelu,
                                bias=b1s[0:m, 6 * l + 2 * c + 1:6 * l + 2 * c + 2]).then_inc(sem["glu_gate"], 1)
                    if l == 0:
                        act.wait_ge(sem["glu_x"], now("glu_x", 1))
                        shifted(xB, "hT", 2)

                act.wait_ge(sem["xn2T_ps"], now("xn2T_ps", 1))
                A(xn2T[:], bank_of("xn2T")[:], ACT.Copy).then_inc(sem["xn2T"], 1)
                for i in range(8):
                    act.wait_ge(sem["att_qk_ps"], now("att_qk_ps", i + 1))
                    A(aqk[:, i, :], bank_of("att_qk", i)[:], ACT.Identity, bias=apb[:, i:i + 1],
                            scale=AD ** -0.5 if i < 4 else 1.0).then_inc(sem["att_qk"], 1)
                act.wait_ge(sem["route_l"], now("route_l", 1))
                act.wait_ge(sem["vec_step"], now("vec_step", ROUTE_EXP))
                A(rsm[:, 4:6, :], rsm[:, 2:4, :], ACT.Exp).then_inc(sem["route_exp"], 1)
                act.wait_ge(sem["att_nmT_ps"], now("att_nmT_ps", 1))
                A(anmT[:], bank_of("att_nmT")[:, 0:256].bitcast(BF16), ACT.Copy).then_inc(sem["att_nmT"], 1)
                for k in range(G * AH):
                    act.wait_ge(sem["att_sT_ps"], now("att_sT_ps", k + 1))
                    if k >= 3:
                        act.wait_ge(sem["att_pv"], now("att_pv", k - 2))
                    A(apr[:, k % 3, :], bank_of("att_sT", k)[:], ACT.Exp).then_inc(sem["att_p"], 1)
                act.wait_ge(sem["att_oT_ps"], now("att_oT_ps", 1))
                A(ftT[:], bank_of("att_oT")[:], ACT.Copy).then_inc(sem["att_oT"], 1)
                for n in range(2 * (EX + 1)):
                    act.wait_ge(sem["moe_g_ps"], now("moe_g_ps", n + 1))
                    if n >= 2:
                        act.wait_ge(sem["moe_h"], now("moe_h", n - 1))
                    A(silu[:, n % 2, :], bank_of("moe_g", n)[:], ACT.Silu).then_inc(sem["moe_silu"], 1)

        @block.vector
        def _(dve):
            V = nc.vector
            dve.wait_ge(loaded, 16 * N_LOADS)
            dve.wait_ge(started, 6)
            done = [0]

            def made(ins):
                done[0] += 1
                ins.then_inc(prep, 1)

            V.memset(bank[0][:, 0:12], 0.0).then_inc(prep_ps, 1)
            made(V.tensor_scalar(fbias[:], W["cols"][:, 0:2], FD ** -0.5, None, ALU.mult))
            made(V.tensor_tensor(projblk[:].rearrange("p (a m) -> p a m", a=4),
                                 W["projT"][:].unsqueeze(1).broadcast_to([P, 4, FM]),
                                 W["block8"][:].rearrange("p (a m) -> p a m", a=4), ALU.mult))
            made(V.tensor_scalar(sqblk[:], W["block8"][:], -0.5, None, ALU.mult))
            for l in range(DEPTH):
                for i in range(4):
                    ins = V.tensor_scalar(rot[:, l, i, :], W["rotary"][:, i, :],
                                          W["cols"][:, 2 + 4 * l + i:3 + 4 * l + i], None, ALU.mult)
                made(ins)
                for i in range(2):
                    ins = V.tensor_copy(
                        wsw[:, l, :].rearrange("p (h a d) -> p h a d", a=2, d=LD // 2)[:, :, i, :],
                        W["wqkv"][:, l, 0:2 * INNER].rearrange("p (h a d) -> p h a d", a=2, d=LD // 2)[:, :, 1 - i, :])
                made(ins)
            for i in range(2):
                made(V.tensor_copy(wpad[:, i, :, :, 0:AD],
                                   W["aw"][:, i, :].rearrange("p (c a d) -> p c a d", c=4, a=4)))
            made(V.tensor_scalar(apb[:, 0:4], W["apb"][:, 0:4], AD ** -0.5, None, ALU.mult))
            made(V.tensor_copy(apb[:, 4:8], W["apb"][:, 4:8]))
            dve.wait_ge(prep_ps, 2)
            for l in range(DEPTH):
                made(V.tensor_scalar(w1s[:, l, :], W["w1"][:, l, :], W["cols"][:, 10 + l:11 + l], None, ALU.mult))
            made(V.tensor_tensor(b1s[:, :], bank[0][:, 0:12], W["b1"][:], ALU.add))
            assert done[0] == 14, done
            made(V.memset(rec[:], 1.0))
            made(V.memset(mv[:], 1.0))

            with dve.Fori(0, TURNS) as it:
                now, prior, freed = counters(dve, it)
                step = [0]

                def link(ins):
                    step[0] += 1
                    ins.then_inc(sem["vec_step"], 1)
                    dve.wait_ge(sem["vec_step"], now("vec_step", step[0]))


                def rsqrt(n):
                    a, y, t = ra[:, 0:n], rs[:, 0:n], rt[:, 0:n]
                    link(V.tensor_scalar(t.bitcast(I32), a.bitcast(I32), 1, None, ALU.logical_shift_right))
                    link(V.tensor_scalar(y.bitcast(I32), t.bitcast(I32), -1, 0x5F3759DF, ALU.mult, ALU.add))
                    for i in range(4):
                        link(V.tensor_tensor(t, a, y, ALU.mult))
                        link(V.tensor_tensor(t, t, y, ALU.mult))
                        link(V.tensor_scalar(t, t, -0.5, 1.5, ALU.mult, ALU.add))
                        if i < 3:
                            link(V.tensor_tensor(y, y, t, ALU.mult))
                    return V.tensor_tensor(y, y, t, ALU.mult)

                def norm(src, dst, eps, name):
                    for j in range(TT):
                        ins = V.bn_stats(st[:, j, :], src[:, j, :])
                    link(ins)
                    V.tensor_copy(rt[:, 0:1], W["ident"][:, 0:1])
                    for j in range(TT):
                        ins = V.bn_aggr(mv[:, j, :], st[:, j, :])
                    link(ins)
                    link(V.tensor_scalar(ra[:, 0:TT], mv[:, :, 1], eps, None, ALU.add))
                    link(rsqrt(TT))
                    for j in range(TT):
                        ins = V.tensor_scalar(dst[:, j, :], src[:, j, :], mv[:, j, 0:1], rs[:, j:j + 1],
                                              ALU.subtract, ALU.mult)
                    ins.then_inc(sem[name], 1)

                def by_row(i):
                    return W["rows"][:, i, :].unsqueeze(1).broadcast_to([P, TT, D])

                dve.wait_ge(x_in_sem, it * 16 + 16)
                dve.wait_ge(sem["xn2T_ps"], prior("xn2T_ps"))
                norm(x_in, xn, 1e-5, "xn")
                dve.wait_ge(sem["favor_v_ps"], now("favor_v_ps", 1))
                dve.wait_ge(sem["att_pv"], prior("att_pv"))
                V.tensor_tensor(fv[:, :, :, 0:FD],
                                      bank_of("favor_v")[:].rearrange("p (t h d) -> p t h d", t=TT, h=FH),
                                      by_row(0).rearrange("p t (h d) -> p t h d", h=FH), ALU.add).then_inc(sem["favor_v"], 1)

                def heads_out(n, b, ps_name, name):
                    o = bank_of(ps_name, b)[:, 0:288].rearrange("p (t h d) -> p t h d", t=2, h=FH)
                    link(V.reciprocal(rec[:, b], o[:, :, :, FD]))
                    V.tensor_tensor(ftm[:, 2 * b:2 * b + 2, :].rearrange("p t (h d) -> p t h d", h=FH),
                                          o[:, :, :, 0:FD], rec[:, b].unsqueeze(3).broadcast_to([P, 2, FH, FD]),
                                          ALU.mult).then_inc(sem[name], 1)

                dve.wait_ge(sem["att_oT_ps"], prior("att_oT_ps"))
                for n in range(G * FH):
                    dve.wait_ge(sem["favor_score_ps"], now("favor_score_ps", n + 1))
                    if n >= 4:
                        dve.wait_ge(sem["favor_pv"], now("favor_pv", n - 3))
                    V.tensor_tensor(fp[:, n % 4, :], bank_of("favor_score", n)[:, 0:384], W["causal"][:],
                                          ALU.mult).then_inc(sem["favor_p"], 1)
                    if n == FH + 4:
                        dve.wait_ge(sem["favor_pv"], now("favor_pv", FH))
                        heads_out(n, 0, "favor_pv", "favor_att")
                dve.wait_ge(sem["favor_pv"], now("favor_pv", 2 * FH))
                heads_out(n, 1, "favor_pv", "favor_att")
                dve.wait_ge(sem["favor_out_ps"], now("favor_out_ps", 1))
                dve.wait_ge(stored, it * 16 + 16)
                V.tensor_tensor(res[:], bank_of("favor_out")[:].rearrange("p (t d) -> p t d", t=TT), xn[:],
                                      ALU.add).then_inc(sem["favor_res"], 1)
                dve.wait_ge(sem["favor_res"], now("favor_res", 1))
                link(V.tensor_tensor(res[:], res[:], by_row(1), ALU.add))
                norm(res, res, 1e-6, "favor_norm")

                for l in range(DEPTH):
                    for c in range(8):
                        n = 8 * l + c
                        tab = lambda i: rot[:, l, 2 * (c // 4) + i, :].unsqueeze(1).broadcast_to([P, G, SEQ])
                        v3 = lambda a: a.rearrange("p (b t) -> p b t", b=G)
                        dve.wait_ge(sem["loc_raw_ps"], now("loc_raw_ps", n + 1))
                        if c == 0:
                            if l:
                                dve.wait_ge(sem["loc_sT_ps"], now("loc_sT_ps", 16))
                            else:
                                dve.wait_ge(sem["loc_sT_ps"], prior("loc_sT_ps"))
                        V.tensor_tensor(v3(lc[:, c, :]), v3(bank_of("loc_raw", n)[:]), tab(0), ALU.mult).then_inc(sem["loc_c"], 1)
                        dve.wait_ge(sem["loc_sw_ps"], now("loc_sw_ps", n + 1))
                        if n >= 2:
                            dve.wait_ge(sem["loc_rot"], now("loc_rot", n - 1))
                        V.tensor_tensor(v3(ls[:, c % 2, :]), v3(bank_of("loc_sw", n)[:]), tab(1), ALU.mult).then_inc(sem["loc_s"], 1)
                    dve.wait_ge(sem["loc_sum_cols"], now("loc_sum_cols", 8 * (l + 1)))
                    V.tensor_scalar(ra[:, 0:64], bank_of("loc_sum", l)[:, 0:64], 1e-24, None, ALU.max).then_inc(sem["loc_sum"], 1)
                    dve.wait_ge(sem["loc_sum"], now("loc_sum", l + 1))
                    rsqrt(64).then_inc(sem["loc_rs"], 1)
                    for c in range(8):
                        n = 8 * l + c
                        dve.wait_ge(sem["loc_rb_ps"], now("loc_rb_ps", n + 1))
                        dve.wait_ge(sem["loc_rot"], now("loc_rot", n + 1))
                        V.tensor_tensor(lc[:, c, :], lc[:, c, :], bank_of("loc_rb", n)[:], ALU.mult).then_inc(sem["loc_qk"], 1)
                    for n in range(8):
                        b, t, hg = n // 4, (n // 2) % 2, n % 2
                        dve.wait_ge(sem["loc_max_ps"], now("loc_max_ps", 8 * l + n + 1))
                        V.tensor_reduce(lmx[:, 2 * b + t, hg:LH:2],
                                              bank_of("loc_max", 8 * l + n)[:].rearrange("p (h k) -> p h k", h=4),
                                              AX.X, ALU.max).then_inc(sem["loc_mx"], 1)
                    dve.wait_ge(sem["loc_mx"], now("loc_mx", 8 * (l + 1)))
                    twice = lmx[:].unsqueeze(2).broadcast_to([P, TT, 2, LH])
                    link(V.tensor_scalar(lnm[:, :, :, 0:LH], twice, -1.0, None, ALU.mult))
                    for g in range(2):
                        ins = V.scalar_tensor_tensor(lnm[:, :, g, LH:2 * LH], lmx[:], -1.0, lnm[:, :, g, 0:LH],
                                                     ALU.mult, ALU.subtract)
                    ins.then_inc(sem["loc_nm"], 1)
                    for b in range(G):
                        for hg in range(2):
                            k = 4 * l + 2 * b + hg
                            dve.wait_ge(sem["loc_pv"], now("loc_pv", 4 * k + 4))
                            for u in range(2):
                                o = bank_of("loc_pv", 2 * k + u)[:, 0:260].rearrange("p (h d) -> p h d", h=4)
                                link(V.reciprocal(rec[:, u, hg, 0:4], o[:, :, LD]))
                                ins = V.tensor_tensor(
                                    lo[:, 2 * b + u, hg * 256:hg * 256 + 256].rearrange("p (h d) -> p h d", h=4),
                                    o[:, :, 0:LD], rec[:, u, hg, 0:4].unsqueeze(2).broadcast_to([P, 4, LD]), ALU.mult)
                            ins.then_inc(sem["loc_o"], 1)
                    dve.wait_ge(sem["loc_wo_ps"], now("loc_wo_ps", l + 1))
                    V.tensor_tensor(xB[:], bank_of("loc_wo", l)[:], (xB if l else xnT)[:], ALU.add).then_inc(sem["loc_x"], 1)
                    dve.wait_ge(sem["glu_mean_ps"], now("glu_mean_ps", l + 1))
                    dve.wait_ge(sem["glu_h"], now("glu_h", 2 * (l + 1)))
                    V.tensor_tensor(cen[:].rearrange("p (b t) -> p b t", b=G), hT[:, :, 0:SEQ],
                                          bank_of("glu_mean", l)[:].rearrange("p (b t) -> p b t", b=G),
                                          ALU.subtract).then_inc(sem["glu_cen"], 1)
                    dve.wait_ge(sem["glu_var_ps"], now("glu_var_ps", l + 1))
                    V.tensor_scalar(ra[:, 0:TT], bank_of("glu_var", l)[:, 0:TT], 1e-5, None, ALU.add).then_inc(sem["glu_var"], 1)
                    dve.wait_ge(sem["glu_var"], now("glu_var", l + 1))
                    rsqrt(TT).then_inc(sem["glu_rs"], 1)
                    dve.wait_ge(sem["glu_rb_ps"], now("glu_rb_ps", l + 1))
                    V.tensor_tensor(cen[:], cen[:], bank_of("glu_rb", l)[:], ALU.mult).then_inc(sem["glu_hn"], 1)
                    for c, (r0, m) in enumerate(HC):
                        n = 3 * l + c
                        dve.wait_ge(sem["glu_a_ps"], now("glu_a_ps", n + 1))
                        dve.wait_ge(sem["glu_gate"], now("glu_gate", n + 1))
                        V.scalar_tensor_tensor(hid[0:m, c, :], bank_of("glu_a", n)[0:m, :],
                                                     b1s[0:m, 6 * l + 2 * c:6 * l + 2 * c + 1],
                                                     gate[0:m, n % 2, :], ALU.add, ALU.mult).then_inc(sem["glu_hid"], 1)
                    dve.wait_ge(sem["glu_out_ps"], now("glu_out_ps", l + 1))
                    V.scalar_tensor_tensor(xB[:], bank_of("glu_out", l)[:], W["cols"][:, 12 + l:13 + l], xB[:],
                                                 ALU.add, ALU.add).then_inc(sem["glu_x"], 1)

                dve.wait_ge(sem["yT_ps"], now("yT_ps", 1))
                dve.wait_ge(sem["favor_done"], now("favor_done", 1))
                V.tensor_tensor(x1[:], x1[:], bank_of("yT")[:].rearrange("p (t d) -> p t d", t=TT), ALU.add).then_inc(sem["x1"], 1)
                dve.wait_ge(sem["x1"], now("x1", 1))
                norm(x1, xn, 1e-5, "xn2")
                dve.wait_ge(sem["att_v_ps"], now("att_v_ps", 1))
                V.tensor_tensor(av[:, :, :, 0:AD],
                                      bank_of("att_v")[:].rearrange("p (t h d) -> p t h d", t=TT, h=AH),
                                      by_row(4).rearrange("p t (h d) -> p t h d", h=AH), ALU.add).then_inc(sem["att_v"], 1)
                dve.wait_ge(sem["route_ps"], now("route_ps", 1))
                R = [route[:, i, :].rearrange("p (t e) -> p t e", t=TT) for i in range(10)]
                wide = lambda a: a.unsqueeze(2).broadcast_to([P, TT, EX])
                rank = W["rank"][:].unsqueeze(1).broadcast_to([P, TT, EX])
                logits, choice, one, two, tmp, wf = R[0], R[1], R[2], R[3], R[4], R[5]
                V.tensor_scalar(logits, bank_of("route")[:, 0:TT * EX].rearrange("p (t e) -> p t e", t=TT),
                                      D ** -0.5, None, ALU.mult).then_inc(sem["route_l"], 1)
                dve.wait_ge(sem["route_l"], now("route_l", 1))
                link(V.tensor_tensor(choice, logits, W["rb"][:].unsqueeze(1).broadcast_to([P, TT, EX]), ALU.add))
                for hot in (one, two):
                    link(V.tensor_reduce(rsm[:, 0, :], choice, AX.X, ALU.max))
                    link(V.tensor_tensor(tmp, choice, wide(rsm[:, 0, :]), ALU.is_equal))
                    link(V.tensor_tensor(tmp, tmp, rank, ALU.mult))
                    link(V.tensor_reduce(rsm[:, 1, :], tmp, AX.X, ALU.max))
                    link(V.tensor_tensor(hot, rank, wide(rsm[:, 1, :]), ALU.is_equal))
                    if hot is one:
                        link(V.scalar_tensor_tensor(choice, one, -3e38, choice, ALU.mult, ALU.add))
                for i, hot in enumerate((one, two)):
                    link(V.tensor_tensor(tmp, hot, logits, ALU.mult))
                    link(V.tensor_reduce(rsm[:, 6 + i, :], tmp, AX.X, ALU.add))
                link(V.tensor_tensor(rsm[:, 0, :], rsm[:, 6, :], rsm[:, 7, :], ALU.max))
                V.tensor_tensor(rsm[:, 2, :], rsm[:, 6, :], rsm[:, 0, :], ALU.subtract)
                link(V.tensor_tensor(rsm[:, 3, :], rsm[:, 7, :], rsm[:, 0, :], ALU.subtract))
                assert step[0] == ROUTE_EXP, step
                dve.wait_ge(sem["route_exp"], now("route_exp", 1))
                link(V.tensor_tensor(rsm[:, 0, :], rsm[:, 4, :], rsm[:, 5, :], ALU.add))
                link(V.reciprocal(rsm[:, 1, :], rsm[:, 0, :]))
                V.tensor_tensor(rsm[:, 6, :], rsm[:, 4, :], rsm[:, 1, :], ALU.mult)
                link(V.tensor_tensor(rsm[:, 7, :], rsm[:, 5, :], rsm[:, 1, :], ALU.mult))
                V.tensor_tensor(one, one, wide(rsm[:, 6, :]), ALU.mult)
                link(V.tensor_tensor(two, two, wide(rsm[:, 7, :]), ALU.mult))
                V.tensor_tensor(wf, one, two, ALU.add).then_inc(sem["route_w"], 1)

                for n in range(G * AH):
                    b, h = divmod(n, AH)
                    dve.wait_ge(sem["att_max_ps"], now("att_max_ps", n + 1))
                    V.tensor_reduce(amx[:, 2 * b:2 * b + 2, h],
                                          bank_of("att_max", n)[:].rearrange("p (t k) -> p t k", t=2),
                                          AX.X, ALU.max).then_inc(sem["att_mx"], 1)
                dve.wait_ge(sem["att_mx"], now("att_mx", 32))
                four = amx[:].unsqueeze(2).broadcast_to([P, TT, 4, AH])
                link(V.tensor_scalar(anm[:, :, :, 0, :], four, -1.0, None, ALU.mult))
                for g in range(4):
                    ins = V.scalar_tensor_tensor(anm[:, :, g, 1, :], amx[:], -1.0, anm[:, :, g, 0, :],
                                                 ALU.mult, ALU.subtract)
                ins.then_inc(sem["att_nm"], 1)
                for b in range(G):
                    dve.wait_ge(sem["att_pv"], now("att_pv", AH * (b + 1)))
                    heads_out(0, b, "att_pv", "att_o")
                link(V.tensor_tensor(moe[:], x1[:], by_row(5), ALU.add))
                dve.wait_ge(sem["route_w"], now("route_w", 1))
                for e in range(EX + 1):
                    for i in range(2):
                        n = 2 * e + i
                        dve.wait_ge(sem["moe_u_ps"], now("moe_u_ps", n + 1))
                        dve.wait_ge(sem["moe_silu"], now("moe_silu", n + 1))
                        if e >= 2:
                            dve.wait_ge(sem["moe_out_ps"], now("moe_out_ps", e - 1))
                        V.tensor_tensor(mh[:, n % 4, :], bank_of("moe_u", n)[:], silu[:, n % 2, :], ALU.mult).then_inc(sem["moe_h"], 1)
                    if e >= 1:
                        dve.wait_ge(sem["moe_out_ps"], now("moe_out_ps", e))
                        if e >= 2:
                            dve.wait_ge(sem["moe_acc"], now("moe_acc", e - 1))
                        for j in range(TT):
                            ins = V.scalar_tensor_tensor(moe[:, j, :], bank_of("moe_out", e - 1)[:, j * P:(j + 1) * P],
                                                         wf[:, j, e - 1:e], moe[:, j, :], ALU.mult, ALU.add)
                        ins.then_inc(sem["moe_acc"], 1)
                dve.wait_ge(sem["final_ps"], now("final_ps", 1))
                dve.wait_ge(sem["moe_acc"], now("moe_acc", 8))
                V.tensor_tensor(res[:], moe[:], bank_of("final")[:].rearrange("p (t d) -> p t d", t=TT),
                                      ALU.add).then_inc(sem["result"], 1)


ROUTE_EXP = 170
COUNTS["loc_sum_cols"] = 16
del COUNTS["loc_sum_ps"]


_WEIGHTS = None


def kernel(**inputs):
    import concourse.bacc as _bacc
    from concourse.bass_utils import run_bass_kernel_spmd as _run

    f = {n: np.asarray(a) for n, a in inputs.items()}

    def g(n):
        return f[n]

    def spread(v):
        return np.broadcast_to(v, (P,) + v.shape)

    def chunks(v, off):
        return [v[off + o:off + o + P] if m == P else np.concatenate([v[off + o:off + o + m], v[off:off + P - m]])
                for o, m in HC]

    a = dict(consts())
    a["fw"] = np.stack([g("L0_attn_" + n) for n in ("q_w", "k_w", "v_w", "out_w")], 1)
    a["projT"] = np.tile(g("L0_attn_proj").T, (P // FD, 1))
    qs, ks = g("L0_ffn_q_scale"), g("L0_ffn_k_scale")
    cols = [g("L0_attn_q_b"), g("L0_attn_k_b")]
    for l in range(DEPTH):
        for s in (qs[l], ks[l]):
            cols.append(np.tile(s, 2))
            cols.append(np.tile(np.roll(s, LD // 2), 2))
    cols += [g("L0_ffn_ln_g")[l] for l in range(DEPTH)]
    cols += [g("L0_ffn_b2")[l] for l in range(DEPTH)]
    cols += [g("L0_ffn_b2")[0]]
    cols += [g("L0_ffn_ln_b")[l] for l in range(DEPTH)]
    a["cols"] = np.stack(cols, 1)
    a["rows"] = spread(np.stack([g("L0_attn_v_b"), g("L0_attn_out_b"), g("L0_attn_gamma"), g("L0_attn_beta"),
                                 g("L1_attn_bv"), g("L1_attn_bo")]))
    a["wqkv"] = g("L0_ffn_wqkv").transpose(1, 0, 2)
    a["wo"] = g("L0_ffn_wo").reshape(DEPTH, 4, P, D).transpose(2, 0, 1, 3)
    a["w1"] = g("L0_ffn_w1").transpose(1, 0, 2)
    b1 = g("L0_ffn_b1")
    a["b1"] = np.stack([c for l in range(DEPTH)
                        for pair in zip(chunks(b1[l], 0), chunks(b1[l], HID)) for c in pair], 1)
    w2 = g("L0_ffn_w2")
    a["w2"] = np.stack([np.stack([w2[l, o:o + P] if m == P else np.concatenate([w2[l, o:o + m], w2[l, :P - m]])
                                  for o, m in HC]) for l in range(DEPTH)]).transpose(2, 0, 1, 3)
    a["aw"] = np.stack([g("L1_attn_" + n).T for n in ("Wq", "Wk", "Wv", "Wo")], 1)
    pads = []
    for n in ("bq", "bk"):
        v = g("L1_attn_" + n).reshape(4, 4, AD)
        full = np.zeros((4, 4, 32), v.dtype)
        full[:, :, :AD] = v
        pads.append(full.reshape(4, P).T)
    a["apb"] = np.concatenate(pads, 1)
    a["wr"] = g("L1_ffn_Wr")
    a["rb"] = spread(g("L1_ffn_rb"))
    for n, e, s in (("mw1", "W1", "Ws1"), ("mw3", "W3", "Ws3")):
        a[n] = np.concatenate([g("L1_ffn_" + e), g("L1_ffn_" + s)[None]]).transpose(1, 0, 2)
    a["mw2"] = np.concatenate([g("L1_ffn_W2"), g("L1_ffn_Ws2")[None]]).reshape(EX + 1, 2, P, D).transpose(2, 0, 1, 3)

    nc = _bacc.Bacc("TRN2", target_bir_lowering=False, num_devices=1)
    arrays, w = {}, {}
    for n, v in a.items():
        v = np.ascontiguousarray(v)
        arrays["in_" + n] = v
        w[n] = nc.dram_tensor("in_" + n, v.shape, mybir.dt.from_np(v.dtype), kind="ExternalInput").ap()
    xs = np.ascontiguousarray(g("L0_attn_x"))
    arrays["in_x"] = xs
    flat = "(i b) (t p) d -> i p (b t) d"
    x = nc.dram_tensor("in_x", xs.shape, F32, kind="ExternalInput").ap()
    out = nc.dram_tensor("out", xs.shape, F32, kind="ExternalOutput").ap()
    x = x.rearrange("n s d -> (n s) d").rearrange("(i j p) d -> i p j d", j=TT, p=P)
    o = out.rearrange("n s d -> (n s) d").rearrange("(i j p) d -> i p j d", j=TT, p=P)
    build(nc, w, x, o)
    r = _run(nc, [arrays], core_ids=[0])
    return r.results[0]["out"]
```

```python
from contextlib import ExitStack

import numpy as np

import concourse.bass as bass
from concourse import mybir

ALU = mybir.AluOpType
ACT = mybir.ActivationFunctionType
AX = mybir.AxisListType
F32 = mybir.dt.float32
BF16 = mybir.dt.bfloat16
I32 = mybir.dt.int32

P = 128
BATCHES, SEQ, D = 16, 256, 128
G = 2
T = G * SEQ
TT = T // P
TURNS = BATCHES // G

FH, FD, FM = 16, 8, 32
LH, LD, WIN, DEPTH = 8, 64, 64, 2
INNER = LH * LD
HID = int(D * 4 * 2 / 3)
HC = [(0, 128), (128, 128), (256, HID - 256)]
AH, AD = 16, 8
EX, EH = 8, 256
NEG = -1e30
LSPAN = 192 + 128

COUNTS = {
    "xnT_ps": 1, "favor_qk_ps": 2, "favor_map_ps": 8, "favor_v_ps": 1, "favor_score_ps": 32,
    "favor_pv": 32, "favor_aT_ps": 1, "favor_out_ps": 1,
    "loc_raw_ps": 16, "loc_sw_ps": 16, "loc_sum_ps": 2, "loc_rT_ps": 2, "loc_rb_ps": 16, "loc_v_ps": 8,
    "loc_max_ps": 16, "loc_nmT_ps": 2, "loc_sT_ps": 32, "loc_pv": 32, "loc_oT_ps": 8, "loc_wo_ps": 2,
    "glu_mean_ps": 2, "glu_var_ps": 2, "glu_rb_ps": 2, "glu_a_ps": 6, "glu_g_ps": 6, "glu_out_ps": 2,
    "yT_ps": 1,
    "xn2T_ps": 1, "att_qk_ps": 2, "att_v_ps": 1, "att_max_ps": 32, "att_nmT_ps": 1, "att_sT_ps": 32,
    "att_pv": 32, "att_oT_ps": 1, "route_ps": 1, "moe_g_ps": 18, "moe_u_ps": 18, "moe_out_ps": 8,
    "final_ps": 1,
    "x_kept": 1, "xnT": 1, "hT": 4, "favor_qk": 2, "favor_sq": 2, "favor_phi": 8, "favor_aT": 1,
    "loc_sq": 16, "loc_rT": 2, "loc_v": 8, "loc_nmT": 2, "loc_p": 32, "loc_oT": 8,
    "glu_h": 4, "glu_sq": 2, "glu_gate": 6,
    "xn2T": 1, "att_qk": 2, "att_part1": 1, "att_part2": 1, "att_nmT": 1, "att_p": 32, "att_oT": 1, "route_exp": 1, "moe_silu": 18,
    "xn": 1, "favor_v": 1, "favor_p": 32, "favor_att": 2, "favor_res": 1, "favor_norm": 1,
    "loc_c": 16, "loc_s": 16, "loc_sum": 2, "loc_rs": 2, "loc_qk": 16, "loc_mx": 16, "loc_nm": 2,
    "loc_o": 8, "loc_x": 2,
    "glu_cen": 2, "glu_var": 2, "glu_rs": 2, "glu_hn": 2, "glu_hid": 6, "glu_x": 2,
    "x1": 1, "xn2": 1, "att_v": 1, "att_mx": 32, "att_nm": 1, "att_o": 2, "route_l": 1, "route_w": 1,
    "moe_h": 18, "moe_acc": 8, "result": 1,
    "vec_step": 158,
    "loc_rot": 16, "favor_done": 1, "pool_step": 2, "att_rest": 1, "att_part3": 1,
    "parts_out": 16, "stack_in": 13 * 16, "nm_out": 16, "nm_in": 16,
}


def consts():
    f, b = np.float32, mybir.dt.np(BF16)
    p = np.arange(P)
    c = {}
    c["ident"] = np.eye(P, dtype=f)
    c["ident4"] = np.tile(np.eye(P), (1, 4)).astype(b)
    c["block8"] = ((p[:, None] % 32) // FD == p[None, :] // FM).astype(f)
    tri = (p[:, None] <= p[None, :]).astype(f)
    c["causal"] = np.concatenate([tri, np.ones((P, P), f), tri], 1)
    q, k = p[:, None], p[None, :]
    ok0 = (k <= q) & (k >= q - WIN)
    r = q % WIN
    ok1 = (k >= r) & (k <= r + WIN)
    c["winmask"] = np.stack([np.where(o, 0, NEG).T for o in (ok0, ok1)], 1).astype(b)
    kk, qq = p[:, None], np.arange(192)[None, :]
    band = np.where((qq >= kk) & (qq <= kk + WIN), 0, NEG)
    c["bandmask"] = np.concatenate([band, band[:, :P]], 1).astype(b)
    s8 = np.zeros((P, LH, P))
    for h in range(LH):
        s8[[LD * (h % 2) + h, LD * (h % 2) + LH + h], h] = 1
    c["sel8"] = s8.astype(b)
    c["half"] = (p[:, None] // LD == np.arange(2)[None, :]).astype(f)
    hs = np.zeros((16, 8, P))
    for i in range(8):
        hs[2 * i, i, :LD] = 1
        hs[2 * i + 1, i, LD:] = 1
    c["headrow"] = np.tile(hs, (3, 1, 1)).astype(b)
    c["ones2"] = np.ones((2, AH * T), b)
    c["mean"] = np.full((P, P), 1.0 / D, f)
    c["rank"] = np.tile(EX - np.arange(EX, dtype=f), (P, 1))
    half = np.arange(0, LD, 2, dtype=f)
    inv = (f(1) / f(10000.0) ** (half / f(LD))).astype(f)
    t = np.arange(SEQ, dtype=f)
    fr = np.concatenate([t[:, None] * inv[None]] * 2, 1)
    base = (half + f(0.4 * LD)) / f(1.4 * LD)
    sc = base[None] ** ((t - SEQ // 2) / f(WIN // 2))[:, None]
    sc = np.concatenate([sc] * 2, 1).astype(f)
    sign = np.where(np.arange(LD) < LD // 2, -1, 1).astype(f)
    tabs = [np.cos(fr) * sc * f(8), np.sin(fr) * sc * sign * f(8), np.cos(fr) / sc, np.sin(fr) / sc * sign]
    c["rotary"] = np.stack([np.tile(x.T, (2, 1)) for x in tabs], 1).astype(f)
    return c


def build(nc, w, x, out):
    with ExitStack() as ctx:
        def sb(name, shape, dt=F32):
            return ctx.enter_context(nc.sbuf_tensor(name, shape, dt))

        bank = [ctx.enter_context(nc.psum_tensor(f"bank{i}", [P, 512], F32)) for i in range(8)]
        sem = {n: ctx.enter_context(nc.semaphore(n)) for n in COUNTS}
        loaded = ctx.enter_context(nc.semaphore("weights_loaded"))
        prep = ctx.enter_context(nc.semaphore("vector_prepared"))
        prep_ps = ctx.enter_context(nc.semaphore("bias_products"))
        started = ctx.enter_context(nc.semaphore("pool_prepared"))
        x_in_sem = ctx.enter_context(nc.semaphore("x_loaded"))
        stored = ctx.enter_context(nc.semaphore("stored"))

        W = {}
        for n, ap in w.items():
            if n != "ones2":
                W[n] = sb("w_" + n, list(ap.shape), ap.dtype)
        fbias = sb("fbias", [P, 2])
        projblk = sb("projblk", [P, P])
        sqblk = sb("sqblk", [P, P])
        rot = sb("rot", [P, DEPTH, 4, SEQ])
        wsw = sb("wsw", [P, DEPTH, 2 * INNER])
        w1s = W["w1"]
        b1s = sb("b1s", [P, DEPTH * 6])
        apb = sb("apb", [P, 2])
        phibias = sb("phibias", [P, 1])

        x_in = sb("x_in", [P, TT, D])
        x1 = sb("x1", [P, TT, D])
        st = sb("st", [P, TT, 6])
        mv = sb("mv", [P, TT, 2])
        xn = sb("xn", [P, TT, D])
        xnT = sb("xnT", [P, T])
        hT = sb("hT", [P, G, SEQ + 1])
        rs = sb("rs", [P, 64])
        ra = sb("ra", [P, 64])
        rt = sb("rt", [P, 64])
        fqs = sb("fqs", [P, 4, T])
        fqk, fsq = fqs[:, 0:2, :], fqs[:, 2:4, :]
        phi = sb("phi", [P, 8, T])
        fv = sb("fv", [P, TT, FH, FD + 1])
        fp = sb("fp", [P, 4, 384])
        rec = sb("rec", [P, G, 2, 16])
        ftm = sb("ftm", [P, TT, D])
        ftT = sb("ftT", [P, T])
        res = sb("res", [P, TT, D])
        lsq = sb("lsq", [P, 2, T])
        lc = sb("lc", [P, 8, T])
        ls = sb("ls", [P, 2, T])
        lsum = sb("lsum", [P, TT * 16])
        lr3 = sb("lr3", [P, TT, 8, 16], BF16)
        lrT = sb("lrT", [48, T], BF16)
        lv = sb("lv", [P, TT, LH, LD + 1])
        lmx = sb("lmx", [P, TT, LH])
        lnm = sb("lnm", [P, TT, 2, LD], BF16)
        lnmT = sb("lnmT", [P, T], BF16)
        lp = fp[:].rearrange("p a b -> p (a b)")[:, 0:4 * LSPAN].rearrange("p (a b) -> p a b", a=4)
        loT = phi[:, 0:4, :]
        lo = phi[:, 4:8, :]
        xB = sb("xB", [P, T])
        cen = sb("cen", [P, T])
        csq = lsq[:, 0, :]
        var = sb("var", [P, TT])
        gate = ls
        hid = fqs[:, 0:3, :]
        xn2T = sb("xn2T", [P, T])
        aqk, arest = fqs[:, 0:2, :], fqs[:, 2:4, :]
        parts = sb("parts", [P, 2, 3, T], BF16)
        qst = phi[:].rearrange("p c t -> p (c t)").bitcast(BF16).rearrange("p (h t) -> p h t", h=AH)
        kst = lc[:].rearrange("p c t -> p (c t)").bitcast(BF16).rearrange("p (h t) -> p h t", h=AH)
        QPART, KPART = (0, 0, 1, 1, 0, 2), (0, 1, 0, 1, 2, 0)
        STACK = AD * len(QPART)
        av = fv
        amx = sb("amx", [P, TT, AH])
        anm = sb("anm", [P, TT, 2, AH], BF16)
        anmT = sb("anmT", [2 * AH, T], BF16)
        apr = fp[:].rearrange("p a b -> p (a b)").rearrange("p (a b) -> p a b", a=3)
        route = sb("route", [P, 10, TT * EX])
        rsm = sb("rsm", [P, 8, TT])
        silu = sb("silu", [P, 2, T])
        mh = sb("mh", [P, 4, T])
        moe = sb("moe", [P, TT, D])

        dparts = nc.dram_tensor("dparts", [2, 3, AH, AD, T], BF16, kind="Internal").ap()
        dnm = nc.dram_tensor("dnm", [2, AH, T], BF16, kind="Internal").ap()

        block = ctx.enter_context(nc.Block())

        FAVOR_AT = {("sums", 0): range(0, 8), ("rT", 0): range(8, 10), ("nm", 0): range(26, 32)}
        FAVOR_AT |= {("rb", c): range(10 + c, 11 + c) for c in range(8)}
        FAVOR_AT |= {("max", c): range(18 + c, 19 + c) for c in range(8)}
        EARLY = 3
        EXPERT_AT = {6 * (e - EARLY) + 5: e for e in range(EARLY, EX)}

        RINGS = {"short": ([], 0, 6), "long": ([], 6, 2)}
        LONG = ("favor_pv", "loc_pv", "att_pv", "loc_sum")

        def job(name, k, freed_by, count):
            RINGS["long" if name in LONG else "short"][0].append((name, k, freed_by, count))

        job("xnT", 0, "hT", 2)
        for i in range(2):
            job("favor_qk", i, "favor_qk", i + 1)
        job("favor_v", 0, "favor_v", 1)

        def favor_jobs(slot, l=0):
            for n in FAVOR_AT[slot] if l == 0 else ():
                if n % FH == 0:
                    job("favor_pv", n // FH, "favor_att", n // FH + 1)
                job("favor_score", n, "favor_p", n + 1)

        def expert_jobs(e):
            for j in range(2):
                job("moe_g", 2 * e + j, "moe_silu", 2 * e + j + 1)
                job("moe_u", 2 * e + j, "moe_h", 2 * e + j + 1)
            if e < EX:
                job("moe_out", e, "moe_acc", e + 1)

        for l in range(DEPTH):
            job("loc_sum", l, "loc_sum", l + 1)
            for c in range(8):
                job("loc_raw", 8 * l + c, "loc_sq", 8 * l + c + 1)
                job("loc_sw", 8 * l + c, "loc_s", 8 * l + c + 1)
                if l == 0:
                    job("favor_map", c, "favor_phi", c + 1)
            for j in range(TT):
                job("loc_v", TT * l + j, "loc_v", TT * l + j + 1)
            favor_jobs(("sums", 0), l)
            job("loc_rT", l, "loc_rT", l + 1)
            favor_jobs(("rT", 0), l)
            for c in range(8):
                job("loc_rb", 8 * l + c, "loc_qk", 8 * l + c + 1)
                favor_jobs(("rb", c), l)
            for j in range(8):
                job("loc_max", 8 * l + j, "loc_mx", 8 * l + j + 1)
                favor_jobs(("max", j), l)
            favor_jobs(("nm", 0), l)
            job("loc_nmT", l, "loc_nmT", l + 1)
            for b in range(G):
                for hg in range(2):
                    job("loc_pv", ((l * G + b) * 2 + hg) * 2, "loc_o", 4 * l + 2 * b + hg + 1)
                    job("loc_pv", ((l * G + b) * 2 + hg) * 2 + 1, "loc_o", 4 * l + 2 * b + hg + 1)
                    for h in range(4):
                        n = (l * G + b) * 8 + hg * 4 + h
                        job("loc_sT", n, "loc_p", n + 1)
                        if n == 6:
                            job("favor_aT", 0, "favor_aT", 1)
                        if n == 10:
                            job("favor_out", 0, "favor_res", 1)
            for c in range(4):
                job("loc_oT", 4 * l + c, "loc_oT", 4 * l + c + 1)
            job("loc_wo", l, "loc_x", l + 1)
            job("glu_mean", l, "glu_cen", l + 1)
            job("glu_var", l, "glu_var", l + 1)
            job("glu_rb", l, "glu_hn", l + 1)
            for c in range(3):
                job("glu_g", 3 * l + c, "glu_gate", 3 * l + c + 1)
                job("glu_a", 3 * l + c, "glu_hid", 3 * l + c + 1)
            job("glu_out", l, "glu_x", l + 1)
        job("yT", 0, "x1", 1)
        job("xn2T", 0, "xn2T", 1)
        for i in range(2):
            job("att_qk", i, "att_qk", i + 1)
        job("route", 0, "route_l", 1)
        job("att_v", 0, "att_v", 1)
        for e in range(EARLY):
            expert_jobs(e)
        for i in range(32):
            job("att_max", i, "att_mx", i + 1)
            if i in EXPERT_AT:
                expert_jobs(EXPERT_AT[i])
        job("att_nmT", 0, "att_nmT", 1)
        expert_jobs(EX)
        for b in range(G):
            job("att_pv", b, "att_o", b + 1)
            for h in range(AH):
                job("att_sT", b * AH + h, "att_p", b * AH + h + 1)
        job("att_oT", 0, "att_oT", 1)
        job("final", 0, "result", 1)
        AT = {(n, k): (i, ring) for ring in RINGS.values() for i, (n, k, _, _) in enumerate(ring[0])}

        def bank_of(name, k=0):
            i, (_, first, size) = AT[name, k]
            return bank[first + i % size]

        def counters(eng, it):
            target = eng.alloc_register("target")

            def value(name, count):
                eng.reg_mul(target, it, COUNTS[name])
                eng.reg_add(target, target, count)
                return target

            def now(name, count):
                return value(name, COUNTS[name] + count)

            def prior(name, count=None):
                return value(name, COUNTS[name] if count is None else count)

            def freed(name, k=0):
                i, (jobs, first, size) = AT[name, k]
                if i >= size:
                    _, _, by, count = jobs[i - size]
                    return sem[by], now(by, count)
                _, _, by, count = jobs[max(j for j in range(len(jobs)) if j % size == i)]
                return sem[by], prior(by, count)

            return now, prior, freed

        @block.sync
        def _(sp):
            for n in COUNTS:
                sp.sem_inc(sem[n], COUNTS[n])
            sp.sem_inc(stored, 16)
            for n, ap in w.items():
                if n != "ones2":
                    sp.dma_start(W[n][:], ap).then_inc(loaded, 16)
            with sp.Fori(0, TURNS) as it:
                now, prior, freed = counters(sp, it)
                src = x[it]
                sp.wait_ge(sem["x_kept"], prior("x_kept"))
                sp.wait_ge(sem["xn"], prior("xn"))
                sp.dma_start(x_in[:], src).then_inc(x_in_sem, 16)
                sp.wait_ge(sem["att_part3"], now("att_part3", 1))
                sp.wait_ge(sem["att_part2"], now("att_part2", 1))
                sp.dma_start(dparts.rearrange("w s h d t -> (h d) w s t"), parts[:]).then_inc(sem["parts_out"], 16)
                sp.wait_ge(sem["parts_out"], now("parts_out", 16))
                for g in range(len(QPART)):
                    for w_, (st_, part) in enumerate(((qst, QPART[g]), (kst, KPART[g]))):
                        sp.dma_start(st_[AD * g:AD * g + AD, :, :],
                                     dparts[w_, part].rearrange("h d t -> d h t")).then_inc(sem["stack_in"], 16)
                sp.dma_start(kst[STACK:STACK + 2, :, :], w["ones2"].rearrange("a (h t) -> a h t", h=AH)).then_inc(
                    sem["stack_in"], 16)
                sp.wait_ge(sem["att_nmT"], now("att_nmT", 1))
                sp.dma_start(dnm.rearrange("a h t -> (a h) t"), anmT[:]).then_inc(sem["nm_out"], 16)
                sp.wait_ge(sem["nm_out"], now("nm_out", 16))
                sp.dma_start(qst[STACK:STACK + 2, :, :], dnm).then_inc(sem["nm_in"], 16)
                dst = out[it]
                sp.wait_ge(sem["result"], now("result", 1))
                sp.dma_start(dst, res[:]).then_inc(stored, 16)
            sp.wait_ge(stored, 16 * (TURNS + 1))

        N_LOADS = len(W)

        @block.gpsimd
        def _(pool):
            pool.wait_ge(loaded, 16 * N_LOADS)
            nc.gpsimd.memset(hT[:], 0.0).then_inc(started, 1)
            nc.gpsimd.memset(fv[:], 1.0).then_inc(started, 1)
            nc.gpsimd.memset(lv[:], 1.0).then_inc(started, 1)
            nc.gpsimd.memset(lnm[:], 0.0).then_inc(started, 1)
            nc.gpsimd.memset(lr3[:], 0.0).then_inc(started, 1)
            nc.gpsimd.memset(phibias[:], -0.5 * float(np.log(FM))).then_inc(started, 1)
            with pool.Fori(0, TURNS) as it:
                now, prior, freed = counters(pool, it)
                def rotate(l):
                    for c in range(8):
                        n = 8 * l + c
                        pool.wait_ge(sem["loc_c"], now("loc_c", n + 1))
                        pool.wait_ge(sem["loc_s"], now("loc_s", n + 1))
                        nc.gpsimd.tensor_tensor(lc[:, c, :], lc[:, c, :], ls[:, c % 2, :],
                                                ALU.add).then_inc(sem["loc_rot"], 1)

                rotate(0)
                pool.wait_ge(sem["favor_norm"], now("favor_norm", 1))
                rows = lambda i: W["rows"][:, i, :].unsqueeze(1).broadcast_to([P, TT, D])
                nc.gpsimd.tensor_tensor(res[:], res[:], rows(2), ALU.mult).then_inc(sem["pool_step"], 1)
                pool.wait_ge(sem["pool_step"], now("pool_step", 1))
                nc.gpsimd.tensor_tensor(res[:], res[:], rows(3), ALU.add).then_inc(sem["pool_step"], 1)
                pool.wait_ge(sem["pool_step"], now("pool_step", 2))
                pool.wait_ge(sem["x_kept"], now("x_kept", 1))
                nc.gpsimd.tensor_tensor(x1[:], x1[:], res[:], ALU.add).then_inc(sem["favor_done"], 1)
                rotate(1)
                pool.wait_ge(sem["att_part1"], now("att_part1", 1))
                nc.gpsimd.tensor_tensor(arest, aqk, parts[:, :, 0, :], ALU.subtract).then_inc(sem["att_rest"], 1)
                pool.wait_ge(sem["att_part2"], now("att_part2", 1))
                nc.gpsimd.tensor_tensor(parts[:, :, 2, :], arest, parts[:, :, 1, :],
                                        ALU.subtract).then_inc(sem["att_part3"], 1)

        @block.tensor
        def _(pe):
            mm = nc.tensor.matmul
            pe.wait_ge(loaded, 16 * N_LOADS)
            pe.wait_ge(prep_ps, 1)
            for l in range(DEPTH):
                for c, (o, m) in enumerate(HC):
                    for g in range(2):
                        last = mm(bank[0][0:m, 6 * l + 2 * c + g:6 * l + 2 * c + g + 1],
                                  W["w1"][:, l, g * HID + o:g * HID + o + m], W["cols"][:, 14 + 1 + l:16 + l],
                                  start=True, stop=True)
            last.then_inc(prep_ps, 1)
            pe.wait_ge(prep, 14)
            pe.wait_ge(started, 6)
            I = W["ident"]
            with pe.Fori(0, TURNS) as it:
                now, prior, freed = counters(pe, it)


                def transpose4(o, src, ready_name, name):
                    for j in range(TT):
                        last = nc.tensor.transpose(o[:, j * P:(j + 1) * P], src[:, j, :], I[:])
                    last.then_inc(sem[name], 1)

                pe.wait_ge(*freed("xnT"))
                o = bank_of("xnT")
                pe.wait_ge(sem["xn"], now("xn", 1))
                transpose4(o, xn, None, "xnT_ps")
                pe.wait_ge(sem["xnT"], now("xnT", 1))
                for i in range(2):
                    pe.wait_ge(*freed("favor_qk", i))
                    o = bank_of("favor_qk", i)
                    mm(o[:], W["fw"][:, i, :], xnT[:], start=True, stop=True).then_inc(sem["favor_qk_ps"], 1)
                pe.wait_ge(*freed("favor_v"))
                o = bank_of("favor_v")
                for j in range(TT):
                    last = mm(o[:, j * P:(j + 1) * P], xnT[:, j * P:(j + 1) * P], W["fw"][:, 2, :],
                              start=True, stop=True)
                last.then_inc(sem["favor_v_ps"], 1)
                def favor_map(i):
                    w_, c = divmod(i, 4)
                    r = slice(32 * c, 32 * c + 32)
                    pe.wait_ge(*freed("favor_map", i))
                    o = bank_of("favor_map", i)
                    if c == 0:
                        pe.wait_ge(sem["favor_qk"], now("favor_qk", w_ + 1))
                        pe.wait_ge(sem["favor_sq"], now("favor_sq", w_ + 1))
                    mm(o[:], projblk[r, :], fqk[r, w_, :], start=True, stop=False)
                    mm(o[:], sqblk[r, :], fsq[r, w_, :], start=False, stop=True).then_inc(sem["favor_map_ps"], 1)

                def favor_score(n):
                    b, h = divmod(n, FH)
                    c, r = h // 4, slice(32 * (h % 4), 32 * (h % 4) + 32)
                    pe.wait_ge(*freed("favor_score", n))
                    o = bank_of("favor_score", n)
                    pe.wait_ge(sem["favor_phi"], now("favor_phi", 8))
                    t = b * SEQ
                    mm(o[:, 0:256], phi[r, 4 + c, t:t + P], phi[r, c, t:t + SEQ], start=True, stop=True)
                    mm(o[:, 256:384], phi[r, 4 + c, t + P:t + SEQ], phi[r, c, t + P:t + SEQ],
                            start=True, stop=True).then_inc(sem["favor_score_ps"], 1)

                def favor_pv(n):
                    b, h = divmod(n, FH)
                    if h == 0:
                        pe.wait_ge(*freed("favor_pv", b))
                        pe.wait_ge(sem["favor_v"], now("favor_v", 1))
                    o = bank_of("favor_pv", b)[:, 0:288].rearrange("p (t h d) -> p t h d", t=2, h=FH)
                    p = fp[:, n % 4, :]
                    pe.wait_ge(sem["favor_p"], now("favor_p", n + 1))
                    mm(o[:, 0, h, :], p[:, 0:P], fv[:, 2 * b, h, :], start=True, stop=True)
                    mm(o[:, 1, h, :], p[:, P:2 * P], fv[:, 2 * b, h, :], start=True, stop=False)
                    mm(o[:, 1, h, :], p[:, 2 * P:3 * P], fv[:, 2 * b + 1, h, :], start=False, stop=True).then_inc(sem["favor_pv"], 1)

                def favor_heads(slot, l=0):
                    for n in FAVOR_AT[slot] if l == 0 else ():
                        favor_score(n)
                        if n >= 2:
                            favor_pv(n - 2)

                def favor_turn():
                    pe.wait_ge(*freed("favor_aT"))
                    o = bank_of("favor_aT")
                    pe.wait_ge(sem["favor_att"], now("favor_att", 2))
                    transpose4(o, ftm, None, "favor_aT_ps")

                def favor_project():
                    pe.wait_ge(*freed("favor_out"))
                    o = bank_of("favor_out")
                    pe.wait_ge(sem["favor_aT"], now("favor_aT", 1))
                    for j in range(TT):
                        last = mm(o[:, j * P:(j + 1) * P], ftT[:, j * P:(j + 1) * P], W["fw"][:, 3, :],
                                  start=True, stop=True)
                    last.then_inc(sem["favor_out_ps"], 1)

                for l in range(DEPTH):
                    h = hT[:, :, 0:SEQ]
                    pe.wait_ge(sem["hT"], now("hT", 2 * (l + 1)))
                    pe.wait_ge(*freed("loc_sum", l))
                    so = bank_of("loc_sum", l)

                    def sums(c):
                        pe.wait_ge(sem["loc_sq"], now("loc_sq", 8 * l + c + 1))
                        for j in range(TT):
                            last = mm(so[:, j * 16 + 2 * c:j * 16 + 2 * c + 2], lsq[:, c % 2, j * P:(j + 1) * P],
                                      W["half"][:], start=True, stop=True)
                        last.then_inc(sem["loc_sum_cols"], 1)

                    for c in range(8):
                        pe.wait_ge(*freed("loc_raw", 8 * l + c))
                        o = bank_of("loc_raw", 8 * l + c)
                        mm(o[:], W["wqkv"][:, l, c * P:(c + 1) * P], h, start=True, stop=True).then_inc(sem["loc_raw_ps"], 1)
                        pe.wait_ge(*freed("loc_sw", 8 * l + c))
                        o = bank_of("loc_sw", 8 * l + c)
                        mm(o[:], wsw[:, l, c * P:(c + 1) * P], h, start=True, stop=True).then_inc(sem["loc_sw_ps"], 1)
                        if l == 0:
                            favor_map(c)
                        if c >= 1:
                            sums(c - 1)
                    sums(7)
                    for j in range(TT):
                        pe.wait_ge(*freed("loc_v", TT * l + j))
                        o = bank_of("loc_v", TT * l + j)
                        b, t = divmod(j, 2)
                        mm(o[:], hT[:, b, t * P:(t + 1) * P], W["wqkv"][:, l, 2 * INNER:3 * INNER],
                                start=True, stop=True).then_inc(sem["loc_v_ps"], 1)
                    favor_heads(("sums", 0), l)
                    pe.wait_ge(*freed("loc_rT", l))
                    o = bank_of("loc_rT", l).bitcast(BF16)
                    pe.wait_ge(sem["loc_rs"], now("loc_rs", l + 1))
                    for j in range(TT):
                        last = nc.tensor.transpose(o[:, j * P:(j + 1) * P],
                                                   lr3[:, j, :, :].rearrange("p a h -> p (a h)"),
                                                   W["ident4"][:, 0:P])
                    last.then_inc(sem["loc_rT_ps"], 1)
                    favor_heads(("rT", 0), l)
                    pe.wait_ge(sem["loc_rT"], now("loc_rT", l + 1))
                    for c in range(8):
                        pe.wait_ge(*freed("loc_rb", 8 * l + c))
                        o = bank_of("loc_rb", 8 * l + c)
                        mm(o[:], W["headrow"][:, c, :], lrT[:], start=True, stop=True).then_inc(sem["loc_rb_ps"], 1)
                        favor_heads(("rb", c), l)
                    pe.wait_ge(sem["loc_qk"], now("loc_qk", 8 * l + 8))
                    for n in range(8):
                        b, t, hg = n // 4, (n // 2) % 2, n % 2
                        pe.wait_ge(*freed("loc_max", 8 * l + n))
                        o = bank_of("loc_max", 8 * l + n)
                        mm(o[:], W["winmask"][:, t, :], W["ident4"][:], start=True, stop=False,
                           skip_group_check=True)
                        for i in range(4):
                            r, c = slice(64 * hg, 64 * hg + 64), i
                            q0 = b * SEQ + t * P
                            oo = o[:, i * P:(i + 1) * P]
                            if t == 0:
                                last = mm(oo, lc[r, c, q0:q0 + P], lc[r, 4 + c, q0:q0 + P],
                                          start=False, stop=True, skip_group_check=True)
                            else:
                                for u in range(2):
                                    k0 = b * SEQ + (u + 1) * WIN
                                    last = mm(oo[u * 64:u * 64 + 64, :],
                                              lc[r, c, q0 + u * 64:q0 + u * 64 + 64], lc[r, 4 + c, k0:k0 + P],
                                              start=False, stop=True, skip_group_check=True)
                        last.then_inc(sem["loc_max_ps"], 1)
                        favor_heads(("max", n), l)
                    favor_heads(("nm", 0), l)
                    pe.wait_ge(*freed("loc_nmT", l))
                    o = bank_of("loc_nmT", l).bitcast(BF16)
                    pe.wait_ge(sem["loc_nm"], now("loc_nm", l + 1))
                    for j in range(TT):
                        last = nc.tensor.transpose(o[:, j * P:(j + 1) * P],
                                                   lnm[:, j, :, :].rearrange("p g h -> p (g h)"),
                                                   W["ident4"][:, 0:P])
                    last.then_inc(sem["loc_nmT_ps"], 1)
                    if l == 0:
                        favor_pv(G * FH - 2)
                        favor_pv(G * FH - 1)
                    pe.wait_ge(sem["loc_nmT"], now("loc_nmT", l + 1))

                    def loc_sT(n):
                        b, hh = divmod(n, LH)
                        k = l * G * LH + n
                        pe.wait_ge(*freed("loc_sT", k))
                        o = bank_of("loc_sT", k)
                        r, c, t = slice(64 * (hh % 2), 64 * (hh % 2) + 64), hh // 2, b * SEQ
                        mm(o[:, 0:LSPAN], W["ident4"][:, 0:P], W["bandmask"][:], start=True, stop=False,
                           skip_group_check=True)
                        for kt, (c0, q0, nq) in enumerate(((0, 0, 192), (192, P, P))):
                            mm(o[:, c0:c0 + nq], W["sel8"][r, hh, :], lnmT[r, t + q0:t + q0 + nq],
                               start=False, stop=False, skip_group_check=True)
                            last = mm(o[:, c0:c0 + nq], lc[r, 4 + c, t + kt * P:t + kt * P + P],
                                      lc[r, c, t + q0:t + q0 + nq], start=False, stop=True, skip_group_check=True)
                        last.then_inc(sem["loc_sT_ps"], 1)

                    def loc_pv(n):
                        b, hh = divmod(n, LH)
                        k, i = l * G * LH + n, hh % 4
                        j0 = ((l * G + b) * 2 + hh // 4) * 2
                        if i == 0:
                            pe.wait_ge(*freed("loc_pv", j0))
                            pe.wait_ge(*freed("loc_pv", j0 + 1))
                        a, z = [bank_of("loc_pv", j0 + u)[:, i * 65:(i + 1) * 65] for u in range(2)]
                        p = lp[:, k % 4, :]
                        pe.wait_ge(sem["loc_p"], now("loc_p", k + 1))
                        pe.wait_ge(sem["loc_v"], now("loc_v", TT * (l + 1)))
                        v0, v1 = lv[:, 2 * b, hh, :], lv[:, 2 * b + 1, hh, :]
                        mm(a, p[:, 0:P], v0, start=True, stop=True)
                        mm(z, p[:, 192:320], v1, start=True, stop=True)
                        mm(z[0:64, :], p[:, P:192], v0, start=False, stop=True, skip_group_check=True).then_inc(sem["loc_pv"], 1)

                    for n in range(G * LH + 2):
                        if n < G * LH:
                            loc_sT(n)
                        if l == 0 and n == 6:
                            favor_turn()
                        if l == 0 and n == 10:
                            favor_project()
                        if n >= 2:
                            loc_pv(n - 2)
                    pe.wait_ge(sem["loc_o"], now("loc_o", 4 * (l + 1)))
                    for c in range(4):
                        pe.wait_ge(*freed("loc_oT", 4 * l + c))
                        o = bank_of("loc_oT", 4 * l + c)
                        for j in range(TT):
                            last = nc.tensor.transpose(o[:, j * P:(j + 1) * P], lo[:, j, c * P:(c + 1) * P], I[:])
                        last.then_inc(sem["loc_oT_ps"], 1)
                    pe.wait_ge(*freed("loc_wo", l))
                    o = bank_of("loc_wo", l)
                    for c in range(4):
                        pe.wait_ge(sem["loc_oT"], now("loc_oT", 4 * l + c + 1))
                        last = mm(o[:], W["wo"][:, l, c, :], loT[:, c, :], start=(c == 0), stop=(c == 3))
                    last.then_inc(sem["loc_wo_ps"], 1)
                    pe.wait_ge(*freed("glu_mean", l))
                    o = bank_of("glu_mean", l)
                    pe.wait_ge(sem["glu_h"], now("glu_h", 2 * (l + 1)))
                    mm(o[:], W["mean"][:], h, start=True, stop=True).then_inc(sem["glu_mean_ps"], 1)
                    pe.wait_ge(*freed("glu_var", l))
                    o = bank_of("glu_var", l)
                    pe.wait_ge(sem["glu_sq"], now("glu_sq", l + 1))
                    for j in range(TT):
                        last = mm(o[:, j:j + 1], csq[:, j * P:(j + 1) * P], W["mean"][:, 0:1], start=True, stop=True)
                    last.then_inc(sem["glu_var_ps"], 1)
                    pe.wait_ge(*freed("glu_rb", l))
                    o = bank_of("glu_rb", l)
                    pe.wait_ge(sem["glu_rs"], now("glu_rs", l + 1))
                    for j in range(TT):
                        last = mm(o[:, j * P:(j + 1) * P], rs[:, j:j + 1].broadcast_to([P, P]), I[:],
                                  start=True, stop=True)
                    last.then_inc(sem["glu_rb_ps"], 1)
                    pe.wait_ge(sem["glu_hn"], now("glu_hn", l + 1))
                    for c, (r0, m) in enumerate(HC):
                        pe.wait_ge(*freed("glu_g", 3 * l + c))
                        o = bank_of("glu_g", 3 * l + c)
                        mm(o[0:m, :], w1s[:, l, HID + r0:HID + r0 + m], cen[:], start=True, stop=True).then_inc(sem["glu_g_ps"], 1)
                        pe.wait_ge(*freed("glu_a", 3 * l + c))
                        o = bank_of("glu_a", 3 * l + c)
                        mm(o[0:m, :], w1s[:, l, r0:r0 + m], cen[:], start=True, stop=True).then_inc(sem["glu_a_ps"], 1)
                    pe.wait_ge(*freed("glu_out", l))
                    o = bank_of("glu_out", l)
                    for c, (r0, m) in enumerate(HC):
                        pe.wait_ge(sem["glu_hid"], now("glu_hid", 3 * l + c + 1))
                        last = mm(o[:], W["w2"][0:m, l, c, :], hid[0:m, c, :], start=(c == 0), stop=(c == 2))
                    last.then_inc(sem["glu_out_ps"], 1)
                pe.wait_ge(*freed("yT"))
                o = bank_of("yT")
                pe.wait_ge(sem["glu_x"], now("glu_x", 2))
                for j in range(TT):
                    last = nc.tensor.transpose(o[:, j * P:(j + 1) * P], xB[:, j * P:(j + 1) * P], I[:])
                last.then_inc(sem["yT_ps"], 1)

                pe.wait_ge(*freed("xn2T"))
                o = bank_of("xn2T")
                pe.wait_ge(sem["xn2"], now("xn2", 1))
                transpose4(o, xn, None, "xn2T_ps")
                pe.wait_ge(sem["xn2T"], now("xn2T", 1))
                for i in range(2):
                    pe.wait_ge(*freed("att_qk", i))
                    o = bank_of("att_qk", i)
                    mm(o[:], W["aw"][:, i, :], xn2T[:], start=True, stop=True).then_inc(sem["att_qk_ps"], 1)
                pe.wait_ge(*freed("route"))
                o = bank_of("route")
                for j in range(TT):
                    last = mm(o[:, j * EX:(j + 1) * EX], xn2T[:, j * P:(j + 1) * P], W["wr"][:],
                              start=True, stop=True)
                last.then_inc(sem["route_ps"], 1)
                pe.wait_ge(*freed("att_v"))
                o = bank_of("att_v")
                for j in range(TT):
                    last = mm(o[:, j * P:(j + 1) * P], xn2T[:, j * P:(j + 1) * P], W["aw"][:, 2, :],
                              start=True, stop=True)
                last.then_inc(sem["att_v_ps"], 1)
                def expert_out(e):
                    out_bank = ("moe_out", e) if e < EX else ("final", 0)
                    pe.wait_ge(*freed(*out_bank))
                    o = bank_of(*out_bank)
                    pe.wait_ge(sem["moe_h"], now("moe_h", 2 * e + 2))
                    if e == EX:
                        pe.wait_ge(sem["att_oT"], now("att_oT", 1))
                    for j in range(TT):
                        t = slice(j * P, (j + 1) * P)
                        if e == EX:
                            mm(o[:, t], ftT[:, t], W["aw"][:, 3, :], start=True, stop=False)
                        for i in range(2):
                            last = mm(o[:, t], mh[:, (2 * e + i) % 4, t], W["mw2"][:, e, i, :],
                                      start=(e < EX and i == 0), stop=(i == 1))
                    last.then_inc(sem["moe_out_ps" if e < EX else "final_ps"], 1)

                def expert_in(e):
                    for i in range(2):
                        pe.wait_ge(*freed("moe_g", 2 * e + i))
                        o = bank_of("moe_g", 2 * e + i)
                        mm(o[:], W["mw3"][:, e, i * P:(i + 1) * P], xn2T[:], start=True, stop=True).then_inc(sem["moe_g_ps"], 1)
                        pe.wait_ge(*freed("moe_u", 2 * e + i))
                        o = bank_of("moe_u", 2 * e + i)
                        mm(o[:], W["mw1"][:, e, i * P:(i + 1) * P], xn2T[:], start=True, stop=True).then_inc(sem["moe_u_ps"], 1)

                for e in range(EARLY):
                    expert_in(e)
                    expert_out(e)
                pe.wait_ge(sem["stack_in"], now("stack_in", 13 * 16))
                for n in range(G * AH):
                    b, h = divmod(n, AH)
                    t = b * SEQ
                    pe.wait_ge(*freed("att_max", n))
                    o = bank_of("att_max", n)
                    for qt in range(2):
                        last = mm(o[:, qt * SEQ:(qt + 1) * SEQ], qst[0:STACK, h, t + qt * P:t + qt * P + P],
                                  kst[0:STACK, h, t:t + SEQ], start=True, stop=True)
                    last.then_inc(sem["att_max_ps"], 1)
                    if n in EXPERT_AT:
                        expert_in(EXPERT_AT[n])
                        expert_out(EXPERT_AT[n])
                pe.wait_ge(*freed("att_nmT"))
                o = bank_of("att_nmT").bitcast(BF16)
                pe.wait_ge(sem["att_nm"], now("att_nm", 1))
                for j in range(TT):
                    last = nc.tensor.transpose(o[0:2 * AH, j * P:(j + 1) * P],
                                               anm[:, j, :, :].rearrange("p a h -> p (a h)"), W["ident4"][:, 0:P])
                last.then_inc(sem["att_nmT_ps"], 1)
                expert_in(EX)
                pe.wait_ge(sem["nm_in"], now("nm_in", 16))

                def att_sT(n):
                    b, h = divmod(n, AH)
                    t = b * SEQ
                    pe.wait_ge(*freed("att_sT", n))
                    o = bank_of("att_sT", n)
                    for kt in range(2):
                        last = mm(o[:, kt * SEQ:(kt + 1) * SEQ], kst[0:STACK + 2, h, t + kt * P:t + kt * P + P],
                                  qst[0:STACK + 2, h, t:t + SEQ], start=True, stop=True)
                    last.then_inc(sem["att_sT_ps"], 1)

                def att_pv(n):
                    b, h = divmod(n, AH)
                    if h == 0:
                        pe.wait_ge(*freed("att_pv", b))
                        pe.wait_ge(sem["att_v"], now("att_v", 1))
                    o = bank_of("att_pv", b)[:, 0:288].rearrange("p (t h d) -> p t h d", t=2, h=AH)
                    pe.wait_ge(sem["att_p"], now("att_p", n + 1))
                    for qt in range(2):
                        for kt in range(2):
                            q0 = kt * SEQ + qt * P
                            last = mm(o[:, qt, h, :], apr[:, n % 3, q0:q0 + P], av[:, 2 * b + kt, h, :],
                                      start=(kt == 0), stop=(kt == 1))
                    last.then_inc(sem["att_pv"], 1)

                for n in range(G * AH + 2):
                    if n < G * AH:
                        att_sT(n)
                    if n >= 2:
                        att_pv(n - 2)
                pe.wait_ge(*freed("att_oT"))
                o = bank_of("att_oT")
                pe.wait_ge(sem["att_o"], now("att_o", 2))
                transpose4(o, ftm, None, "att_oT_ps")
                expert_out(EX)


        @block.scalar
        def _(act):
            A = nc.scalar.activation
            act.wait_ge(prep, 14)
            act.wait_ge(started, 6)
            with act.Fori(0, TURNS) as it:
                now, prior, freed = counters(act, it)


                def shifted(src, name, k):
                    A(hT[0:64, :, 0:SEQ], src[0:64, :].rearrange("p (b t) -> p b t", b=G), ACT.Copy).then_inc(sem[name], 1)
                    A(hT[64:P, :, 1:SEQ + 1], src[64:P, :].rearrange("p (b t) -> p b t", b=G), ACT.Copy).then_inc(sem[name], 1)

                act.wait_ge(x_in_sem, it * 16 + 16)
                act.wait_ge(sem["result"], prior("result"))
                A(x1[:], x_in[:], ACT.Copy).then_inc(sem["x_kept"], 1)
                act.wait_ge(sem["xnT_ps"], now("xnT_ps", 1))
                act.wait_ge(sem["glu_x"], prior("glu_x"))
                A(xnT[:], bank_of("xnT")[:], ACT.Copy).then_inc(sem["xnT"], 1)
                shifted(bank_of("xnT"), "hT", 0)
                for i in range(2):
                    act.wait_ge(sem["favor_qk_ps"], now("favor_qk_ps", i + 1))
                    A(fqk[:, i, :], bank_of("favor_qk", i)[:], ACT.Identity, bias=fbias[:, i:i + 1],
                            scale=FD ** -0.5).then_inc(sem["favor_qk"], 1)
                for i in range(2):
                    act.wait_ge(sem["favor_qk"], now("favor_qk", i + 1))
                    A(fsq[:, i, :], fqk[:, i, :], ACT.Square).then_inc(sem["favor_sq"], 1)
                for l in range(DEPTH):
                    for c in range(8):
                        n = 8 * l + c
                        act.wait_ge(sem["loc_raw_ps"], now("loc_raw_ps", n + 1))
                        act.wait_ge(sem["loc_c"], now("loc_c", n + 1))
                        if n >= 2:
                            act.wait_ge(sem["loc_sum_cols"], now("loc_sum_cols", n - 1))
                        A(lsq[:, c % 2, :], bank_of("loc_raw", n)[:], ACT.Square).then_inc(sem["loc_sq"], 1)
                        if l == 0:
                            if c == 0:
                                act.wait_ge(sem["att_sT_ps"], prior("att_sT_ps"))
                            act.wait_ge(sem["favor_map_ps"], now("favor_map_ps", c + 1))
                            A(phi[:, c, :], bank_of("favor_map", c)[:], ACT.Exp, bias=phibias[:, 0:1]).then_inc(
                                sem["favor_phi"], 1)
                    for j in range(TT):
                        n = TT * l + j
                        act.wait_ge(sem["loc_v_ps"], now("loc_v_ps", n + 1))
                        if l:
                            act.wait_ge(sem["loc_pv"], now("loc_pv", 16))
                        A(lv[:, j, :, 0:LD], bank_of("loc_v", n)[:].rearrange("p (h d) -> p h d", h=LH),
                                ACT.Copy).then_inc(sem["loc_v"], 1)
                    act.wait_ge(sem["loc_rT_ps"], now("loc_rT_ps", l + 1))
                    A(lrT[:], bank_of("loc_rT", l)[0:48, 0:256].bitcast(BF16), ACT.Copy).then_inc(sem["loc_rT"], 1)
                    act.wait_ge(sem["loc_nmT_ps"], now("loc_nmT_ps", l + 1))
                    A(lnmT[:], bank_of("loc_nmT", l)[:, 0:256].bitcast(BF16), ACT.Copy).then_inc(sem["loc_nmT"], 1)
                    for k in range(16 * l, 16 * l + 16):
                        act.wait_ge(sem["loc_sT_ps"], now("loc_sT_ps", k + 1))
                        if k >= 4:
                            act.wait_ge(sem["loc_pv"], now("loc_pv", k - 3))
                        A(lp[:, k % 4, :], bank_of("loc_sT", k)[:, 0:LSPAN], ACT.Exp).then_inc(sem["loc_p"], 1)
                        if k == 6:
                            act.wait_ge(sem["favor_aT_ps"], now("favor_aT_ps", 1))
                            act.wait_ge(sem["final_ps"], prior("final_ps"))
                            A(ftT[:], bank_of("favor_aT")[:], ACT.Copy).then_inc(sem["favor_aT"], 1)
                    for c in range(4):
                        act.wait_ge(sem["loc_oT_ps"], now("loc_oT_ps", 4 * l + c + 1))
                        if l:
                            act.wait_ge(sem["loc_wo_ps"], now("loc_wo_ps", 1))
                        A(loT[:, c, :], bank_of("loc_oT", 4 * l + c)[:], ACT.Copy).then_inc(sem["loc_oT"], 1)
                    act.wait_ge(sem["loc_x"], now("loc_x", l + 1))
                    shifted(xB, "glu_h", l)
                    act.wait_ge(sem["glu_cen"], now("glu_cen", l + 1))
                    A(csq, cen[:], ACT.Square).then_inc(sem["glu_sq"], 1)
                    for c, (r0, m) in enumerate(HC):
                        n = 3 * l + c
                        act.wait_ge(sem["glu_g_ps"], now("glu_g_ps", n + 1))
                        if n >= 2:
                            act.wait_ge(sem["glu_hid"], now("glu_hid", n - 1))
                        A(gate[0:m, n % 2, :], bank_of("glu_g", n)[0:m, :], ACT.Gelu,
                                bias=b1s[0:m, 6 * l + 2 * c + 1:6 * l + 2 * c + 2]).then_inc(sem["glu_gate"], 1)
                    if l == 0:
                        act.wait_ge(sem["glu_x"], now("glu_x", 1))
                        shifted(xB, "hT", 2)

                act.wait_ge(sem["xn2T_ps"], now("xn2T_ps", 1))
                A(xn2T[:], bank_of("xn2T")[:], ACT.Copy).then_inc(sem["xn2T"], 1)
                for i in range(2):
                    act.wait_ge(sem["att_qk_ps"], now("att_qk_ps", i + 1))
                    A(aqk[:, i, :], bank_of("att_qk", i)[:], ACT.Identity, bias=apb[:, i:i + 1],
                      scale=(AD ** -0.5, 1.0)[i]).then_inc(sem["att_qk"], 1)
                act.wait_ge(sem["att_qk"], now("att_qk", 2))
                act.wait_ge(sem["parts_out"], prior("parts_out"))
                A(parts[:, :, 0, :], aqk, ACT.Copy).then_inc(sem["att_part1"], 1)
                act.wait_ge(sem["att_rest"], now("att_rest", 1))
                A(parts[:, :, 1, :], arest, ACT.Copy).then_inc(sem["att_part2"], 1)
                act.wait_ge(sem["route_l"], now("route_l", 1))
                act.wait_ge(sem["vec_step"], now("vec_step", ROUTE_EXP))
                A(rsm[:, 4:6, :], rsm[:, 2:4, :], ACT.Exp).then_inc(sem["route_exp"], 1)
                for n in range(2 * EX):
                    act.wait_ge(sem["moe_g_ps"], now("moe_g_ps", n + 1))
                    if n >= 2:
                        act.wait_ge(sem["moe_h"], now("moe_h", n - 1))
                    A(silu[:, n % 2, :], bank_of("moe_g", n)[:], ACT.Silu).then_inc(sem["moe_silu"], 1)
                act.wait_ge(sem["att_nmT_ps"], now("att_nmT_ps", 1))
                act.wait_ge(sem["nm_out"], prior("nm_out"))
                A(anmT[:], bank_of("att_nmT")[0:2 * AH, 0:256].bitcast(BF16), ACT.Copy).then_inc(sem["att_nmT"], 1)
                for n in range(2 * EX, 2 * EX + 2):
                    act.wait_ge(sem["moe_g_ps"], now("moe_g_ps", n + 1))
                    if n >= 2:
                        act.wait_ge(sem["moe_h"], now("moe_h", n - 1))
                    A(silu[:, n % 2, :], bank_of("moe_g", n)[:], ACT.Silu).then_inc(sem["moe_silu"], 1)
                for k in range(G * AH):
                    act.wait_ge(sem["att_sT_ps"], now("att_sT_ps", k + 1))
                    if k >= 3:
                        act.wait_ge(sem["att_pv"], now("att_pv", k - 2))
                    A(apr[:, k % 3, :], bank_of("att_sT", k)[:], ACT.Exp).then_inc(sem["att_p"], 1)
                act.wait_ge(sem["att_oT_ps"], now("att_oT_ps", 1))
                A(ftT[:], bank_of("att_oT")[:], ACT.Copy).then_inc(sem["att_oT"], 1)
        @block.vector
        def _(dve):
            V = nc.vector
            dve.wait_ge(loaded, 16 * N_LOADS)
            dve.wait_ge(started, 6)
            done = [0]

            def made(ins):
                done[0] += 1
                ins.then_inc(prep, 1)

            V.memset(bank[0][:, 0:12], 0.0).then_inc(prep_ps, 1)
            made(V.tensor_scalar(fbias[:], W["cols"][:, 0:2], FD ** -0.5, None, ALU.mult))
            made(V.tensor_tensor(projblk[:].rearrange("p (a m) -> p a m", a=4),
                                 W["projT"][:].unsqueeze(1).broadcast_to([P, 4, FM]),
                                 W["block8"][:].rearrange("p (a m) -> p a m", a=4), ALU.mult))
            made(V.tensor_scalar(sqblk[:], W["block8"][:], -0.5, None, ALU.mult))
            for l in range(DEPTH):
                for i in range(4):
                    ins = V.tensor_scalar(rot[:, l, i, :], W["rotary"][:, i, :],
                                          W["cols"][:, 2 + 4 * l + i:3 + 4 * l + i], None, ALU.mult)
                made(ins)
                for i in range(2):
                    ins = V.tensor_copy(
                        wsw[:, l, :].rearrange("p (h a d) -> p h a d", a=2, d=LD // 2)[:, :, i, :],
                        W["wqkv"][:, l, 0:2 * INNER].rearrange("p (h a d) -> p h a d", a=2, d=LD // 2)[:, :, 1 - i, :])
                made(ins)
            made(V.tensor_scalar(apb[:, 0:1], W["cols"][:, 17:18], AD ** -0.5, None, ALU.mult))
            made(V.tensor_copy(apb[:, 1:2], W["cols"][:, 18:19]))
            dve.wait_ge(prep_ps, 2)
            for l in range(DEPTH):
                made(V.tensor_scalar(w1s[:, l, :], W["w1"][:, l, :], W["cols"][:, 10 + l:11 + l], None, ALU.mult))
            made(V.tensor_tensor(b1s[:, :], bank[0][:, 0:12], W["b1"][:], ALU.add))
            assert done[0] == 12, done
            made(V.memset(rec[:], 1.0))
            made(V.memset(mv[:], 1.0))

            with dve.Fori(0, TURNS) as it:
                now, prior, freed = counters(dve, it)
                step = [0]

                def link(ins):
                    step[0] += 1
                    ins.then_inc(sem["vec_step"], 1)
                    dve.wait_ge(sem["vec_step"], now("vec_step", step[0]))


                def rsqrt(n):
                    a, y, t = ra[:, 0:n], rs[:, 0:n], rt[:, 0:n]
                    link(V.tensor_scalar(t.bitcast(I32), a.bitcast(I32), 1, None, ALU.logical_shift_right))
                    link(V.tensor_scalar(y.bitcast(I32), t.bitcast(I32), -1, 0x5F3759DF, ALU.mult, ALU.add))
                    for i in range(3):
                        link(V.tensor_tensor(t, a, y, ALU.mult))
                        link(V.tensor_tensor(t, t, y, ALU.mult))
                        link(V.tensor_scalar(t, t, -0.5, 1.5, ALU.mult, ALU.add))
                        if i < 2:
                            link(V.tensor_tensor(y, y, t, ALU.mult))
                    return V.tensor_tensor(y, y, t, ALU.mult)

                def norm(src, dst, eps, name):
                    for j in range(TT):
                        ins = V.bn_stats(st[:, j, :], src[:, j, :])
                    link(ins)
                    V.tensor_copy(rt[:, 0:1], W["ident"][:, 0:1])
                    for j in range(TT):
                        ins = V.bn_aggr(mv[:, j, :], st[:, j, :])
                    link(ins)
                    link(V.tensor_scalar(ra[:, 0:TT], mv[:, :, 1], eps, None, ALU.add))
                    link(rsqrt(TT))
                    for j in range(TT):
                        ins = V.tensor_scalar(dst[:, j, :], src[:, j, :], mv[:, j, 0:1], rs[:, j:j + 1],
                                              ALU.subtract, ALU.mult)
                    ins.then_inc(sem[name], 1)

                def by_row(i):
                    return W["rows"][:, i, :].unsqueeze(1).broadcast_to([P, TT, D])

                dve.wait_ge(x_in_sem, it * 16 + 16)
                dve.wait_ge(sem["xn2T_ps"], prior("xn2T_ps"))
                norm(x_in, xn, 1e-5, "xn")
                dve.wait_ge(sem["favor_v_ps"], now("favor_v_ps", 1))
                dve.wait_ge(sem["att_pv"], prior("att_pv"))
                V.tensor_tensor(fv[:, :, :, 0:FD],
                                      bank_of("favor_v")[:].rearrange("p (t h d) -> p t h d", t=TT, h=FH),
                                      by_row(0).rearrange("p t (h d) -> p t h d", h=FH), ALU.add).then_inc(sem["favor_v"], 1)

                def heads_out(n, b, ps_name, name):
                    o = bank_of(ps_name, b)[:, 0:288].rearrange("p (t h d) -> p t h d", t=2, h=FH)
                    link(V.reciprocal(rec[:, b], o[:, :, :, FD]))
                    V.tensor_tensor(ftm[:, 2 * b:2 * b + 2, :].rearrange("p t (h d) -> p t h d", h=FH),
                                          o[:, :, :, 0:FD], rec[:, b].unsqueeze(3).broadcast_to([P, 2, FH, FD]),
                                          ALU.mult).then_inc(sem[name], 1)

                dve.wait_ge(sem["att_oT_ps"], prior("att_oT_ps"))
                def favor_heads(slot, l=0):
                    for n in FAVOR_AT[slot] if l == 0 else ():
                        dve.wait_ge(sem["favor_score_ps"], now("favor_score_ps", n + 1))
                        if n >= 4:
                            dve.wait_ge(sem["favor_pv"], now("favor_pv", n - 3))
                        V.tensor_tensor(fp[:, n % 4, :], bank_of("favor_score", n)[:, 0:384], W["causal"][:],
                                        ALU.mult).then_inc(sem["favor_p"], 1)
                        if n == FH + 4:
                            dve.wait_ge(sem["favor_pv"], now("favor_pv", FH))
                            heads_out(n, 0, "favor_pv", "favor_att")

                for l in range(DEPTH):
                    for c in range(8):
                        n = 8 * l + c
                        tab = lambda i: rot[:, l, 2 * (c // 4) + i, :].unsqueeze(1).broadcast_to([P, G, SEQ])
                        v3 = lambda a: a.rearrange("p (b t) -> p b t", b=G)
                        dve.wait_ge(sem["loc_raw_ps"], now("loc_raw_ps", n + 1))
                        if c == 0:
                            if l:
                                dve.wait_ge(sem["loc_sT_ps"], now("loc_sT_ps", 16))
                            else:
                                dve.wait_ge(sem["att_sT_ps"], prior("att_sT_ps"))
                        V.tensor_tensor(v3(lc[:, c, :]), v3(bank_of("loc_raw", n)[:]), tab(0), ALU.mult).then_inc(sem["loc_c"], 1)
                        dve.wait_ge(sem["loc_sw_ps"], now("loc_sw_ps", n + 1))
                        if n >= 2:
                            dve.wait_ge(sem["loc_rot"], now("loc_rot", n - 1))
                        V.tensor_tensor(v3(ls[:, c % 2, :]), v3(bank_of("loc_sw", n)[:]), tab(1), ALU.mult).then_inc(sem["loc_s"], 1)
                    dve.wait_ge(sem["loc_sum_cols"], now("loc_sum_cols", 8 * (l + 1)))
                    V.tensor_scalar(ra[:, 0:64], bank_of("loc_sum", l)[:, 0:64], 1e-24, None, ALU.max).then_inc(sem["loc_sum"], 1)
                    dve.wait_ge(sem["loc_sum"], now("loc_sum", l + 1))
                    link(rsqrt(64))
                    r3, rest = rs[:, 0:64].rearrange("p (j h) -> p j h", j=TT), ra[:, 0:64].rearrange(
                        "p (j h) -> p j h", j=TT)
                    link(V.tensor_copy(lr3[:, :, 0, :], r3))
                    link(V.tensor_tensor(rest, r3, lr3[:, :, 0, :], ALU.subtract))
                    link(V.tensor_copy(lr3[:, :, 1, :], rest))
                    V.tensor_tensor(lr3[:, :, 2, :], rest, lr3[:, :, 1, :], ALU.subtract).then_inc(sem["loc_rs"], 1)
                    favor_heads(("sums", 0), l)
                    favor_heads(("rT", 0), l)
                    for c in range(8):
                        n = 8 * l + c
                        dve.wait_ge(sem["loc_rb_ps"], now("loc_rb_ps", n + 1))
                        dve.wait_ge(sem["loc_rot"], now("loc_rot", n + 1))
                        V.tensor_tensor(lc[:, c, :], lc[:, c, :], bank_of("loc_rb", n)[:], ALU.mult).then_inc(sem["loc_qk"], 1)
                        favor_heads(("rb", c), l)
                    for n in range(8):
                        b, t, hg = n // 4, (n // 2) % 2, n % 2
                        dve.wait_ge(sem["loc_max_ps"], now("loc_max_ps", 8 * l + n + 1))
                        V.tensor_reduce(lmx[:, 2 * b + t, hg:LH:2],
                                              bank_of("loc_max", 8 * l + n)[:].rearrange("p (h k) -> p h k", h=4),
                                              AX.X, ALU.max).then_inc(sem["loc_mx"], 1)
                        favor_heads(("max", n), l)
                    favor_heads(("nm", 0), l)
                    dve.wait_ge(sem["loc_mx"], now("loc_mx", 8 * (l + 1)))
                    twice = lmx[:].unsqueeze(2).broadcast_to([P, TT, 2, LH])
                    link(V.tensor_scalar(lnm[:, :, :, 0:LH], twice, -1.0, None, ALU.mult))
                    for g in range(2):
                        ins = V.scalar_tensor_tensor(lnm[:, :, g, LH:2 * LH], lmx[:], -1.0, lnm[:, :, g, 0:LH],
                                                     ALU.mult, ALU.subtract)
                    ins.then_inc(sem["loc_nm"], 1)
                    if l == 0:
                        dve.wait_ge(sem["favor_pv"], now("favor_pv", 2 * FH))
                        heads_out(n, 1, "favor_pv", "favor_att")
                    for b in range(G):
                        for hg in range(2):
                            k = 4 * l + 2 * b + hg
                            dve.wait_ge(sem["loc_pv"], now("loc_pv", 4 * k + 4))
                            for u in range(2):
                                o = bank_of("loc_pv", 2 * k + u)[:, 0:260].rearrange("p (h d) -> p h d", h=4)
                                link(V.reciprocal(rec[:, u, hg, 0:4], o[:, :, LD]))
                                ins = V.tensor_tensor(
                                    lo[:, 2 * b + u, hg * 256:hg * 256 + 256].rearrange("p (h d) -> p h d", h=4),
                                    o[:, :, 0:LD], rec[:, u, hg, 0:4].unsqueeze(2).broadcast_to([P, 4, LD]), ALU.mult)
                            ins.then_inc(sem["loc_o"], 1)
                            if k == 1:
                                dve.wait_ge(sem["favor_out_ps"], now("favor_out_ps", 1))
                                dve.wait_ge(stored, it * 16 + 16)
                                V.tensor_tensor(res[:], bank_of("favor_out")[:].rearrange("p (t d) -> p t d", t=TT), xn[:],
                                                      ALU.add).then_inc(sem["favor_res"], 1)
                                dve.wait_ge(sem["favor_res"], now("favor_res", 1))
                                link(V.tensor_tensor(res[:], res[:], by_row(1), ALU.add))
                                norm(res, res, 1e-6, "favor_norm")
                    dve.wait_ge(sem["loc_wo_ps"], now("loc_wo_ps", l + 1))
                    V.tensor_tensor(xB[:], bank_of("loc_wo", l)[:], (xB if l else xnT)[:], ALU.add).then_inc(sem["loc_x"], 1)
                    dve.wait_ge(sem["glu_mean_ps"], now("glu_mean_ps", l + 1))
                    dve.wait_ge(sem["glu_h"], now("glu_h", 2 * (l + 1)))
                    V.tensor_tensor(cen[:].rearrange("p (b t) -> p b t", b=G), hT[:, :, 0:SEQ],
                                          bank_of("glu_mean", l)[:].rearrange("p (b t) -> p b t", b=G),
                                          ALU.subtract).then_inc(sem["glu_cen"], 1)
                    dve.wait_ge(sem["glu_var_ps"], now("glu_var_ps", l + 1))
                    V.tensor_scalar(ra[:, 0:TT], bank_of("glu_var", l)[:, 0:TT], 1e-5, None, ALU.add).then_inc(sem["glu_var"], 1)
                    dve.wait_ge(sem["glu_var"], now("glu_var", l + 1))
                    rsqrt(TT).then_inc(sem["glu_rs"], 1)
                    dve.wait_ge(sem["glu_rb_ps"], now("glu_rb_ps", l + 1))
                    V.tensor_tensor(cen[:], cen[:], bank_of("glu_rb", l)[:], ALU.mult).then_inc(sem["glu_hn"], 1)
                    for c, (r0, m) in enumerate(HC):
                        n = 3 * l + c
                        dve.wait_ge(sem["glu_a_ps"], now("glu_a_ps", n + 1))
                        dve.wait_ge(sem["glu_gate"], now("glu_gate", n + 1))
                        V.scalar_tensor_tensor(hid[0:m, c, :], bank_of("glu_a", n)[0:m, :],
                                                     b1s[0:m, 6 * l + 2 * c:6 * l + 2 * c + 1],
                                                     gate[0:m, n % 2, :], ALU.add, ALU.mult).then_inc(sem["glu_hid"], 1)
                    dve.wait_ge(sem["glu_out_ps"], now("glu_out_ps", l + 1))
                    V.scalar_tensor_tensor(xB[:], bank_of("glu_out", l)[:], W["cols"][:, 12 + l:13 + l], xB[:],
                                                 ALU.add, ALU.add).then_inc(sem["glu_x"], 1)

                dve.wait_ge(sem["yT_ps"], now("yT_ps", 1))
                dve.wait_ge(sem["favor_done"], now("favor_done", 1))
                V.tensor_tensor(x1[:], x1[:], bank_of("yT")[:].rearrange("p (t d) -> p t d", t=TT), ALU.add).then_inc(sem["x1"], 1)
                dve.wait_ge(sem["x1"], now("x1", 1))
                norm(x1, xn, 1e-5, "xn2")
                dve.wait_ge(sem["att_v_ps"], now("att_v_ps", 1))
                V.tensor_tensor(av[:, :, :, 0:AD],
                                      bank_of("att_v")[:].rearrange("p (t h d) -> p t h d", t=TT, h=AH),
                                      by_row(4).rearrange("p t (h d) -> p t h d", h=AH), ALU.add).then_inc(sem["att_v"], 1)
                dve.wait_ge(sem["route_ps"], now("route_ps", 1))
                R = [route[:, i, :].rearrange("p (t e) -> p t e", t=TT) for i in range(10)]
                wide = lambda a: a.unsqueeze(2).broadcast_to([P, TT, EX])
                rank = W["rank"][:].unsqueeze(1).broadcast_to([P, TT, EX])
                logits, choice, one, two, tmp, wf = R[0], R[1], R[2], R[3], R[4], R[5]
                V.tensor_scalar(logits, bank_of("route")[:, 0:TT * EX].rearrange("p (t e) -> p t e", t=TT),
                                      D ** -0.5, None, ALU.mult).then_inc(sem["route_l"], 1)
                dve.wait_ge(sem["route_l"], now("route_l", 1))
                link(V.tensor_tensor(choice, logits, W["rb"][:].unsqueeze(1).broadcast_to([P, TT, EX]), ALU.add))
                for hot in (one, two):
                    link(V.tensor_reduce(rsm[:, 0, :], choice, AX.X, ALU.max))
                    link(V.tensor_tensor(tmp, choice, wide(rsm[:, 0, :]), ALU.is_equal))
                    link(V.tensor_tensor(tmp, tmp, rank, ALU.mult))
                    link(V.tensor_reduce(rsm[:, 1, :], tmp, AX.X, ALU.max))
                    link(V.tensor_tensor(hot, rank, wide(rsm[:, 1, :]), ALU.is_equal))
                    if hot is one:
                        link(V.scalar_tensor_tensor(choice, one, -3e38, choice, ALU.mult, ALU.add))
                for i, hot in enumerate((one, two)):
                    link(V.tensor_tensor(tmp, hot, logits, ALU.mult))
                    link(V.tensor_reduce(rsm[:, 6 + i, :], tmp, AX.X, ALU.add))
                link(V.tensor_tensor(rsm[:, 0, :], rsm[:, 6, :], rsm[:, 7, :], ALU.max))
                V.tensor_tensor(rsm[:, 2, :], rsm[:, 6, :], rsm[:, 0, :], ALU.subtract)
                link(V.tensor_tensor(rsm[:, 3, :], rsm[:, 7, :], rsm[:, 0, :], ALU.subtract))
                assert step[0] == ROUTE_EXP, step
                dve.wait_ge(sem["route_exp"], now("route_exp", 1))
                link(V.tensor_tensor(rsm[:, 0, :], rsm[:, 4, :], rsm[:, 5, :], ALU.add))
                link(V.reciprocal(rsm[:, 1, :], rsm[:, 0, :]))
                V.tensor_tensor(rsm[:, 6, :], rsm[:, 4, :], rsm[:, 1, :], ALU.mult)
                link(V.tensor_tensor(rsm[:, 7, :], rsm[:, 5, :], rsm[:, 1, :], ALU.mult))
                V.tensor_tensor(one, one, wide(rsm[:, 6, :]), ALU.mult)
                link(V.tensor_tensor(two, two, wide(rsm[:, 7, :]), ALU.mult))
                V.tensor_tensor(wf, one, two, ALU.add).then_inc(sem["route_w"], 1)

                link(V.tensor_tensor(moe[:], x1[:], by_row(5), ALU.add))

                def expert_hidden(e):
                    for i in range(2):
                        n = 2 * e + i
                        dve.wait_ge(sem["moe_u_ps"], now("moe_u_ps", n + 1))
                        dve.wait_ge(sem["moe_silu"], now("moe_silu", n + 1))
                        if e >= 2:
                            dve.wait_ge(sem["moe_out_ps"], now("moe_out_ps", e - 1))
                        V.tensor_tensor(mh[:, n % 4, :], bank_of("moe_u", n)[:], silu[:, n % 2, :],
                                        ALU.mult).then_inc(sem["moe_h"], 1)

                def expert_add(e):
                    dve.wait_ge(sem["moe_out_ps"], now("moe_out_ps", e + 1))
                    if e == 0:
                        dve.wait_ge(sem["route_w"], now("route_w", 1))
                    else:
                        dve.wait_ge(sem["moe_acc"], now("moe_acc", e))
                    for j in range(TT):
                        ins = V.scalar_tensor_tensor(moe[:, j, :], bank_of("moe_out", e)[:, j * P:(j + 1) * P],
                                                     wf[:, j, e:e + 1], moe[:, j, :], ALU.mult, ALU.add)
                    ins.then_inc(sem["moe_acc"], 1)

                for e in range(EARLY):
                    expert_hidden(e)
                    expert_add(e)
                for n in range(G * AH):
                    b, h = divmod(n, AH)
                    dve.wait_ge(sem["att_max_ps"], now("att_max_ps", n + 1))
                    V.tensor_reduce(amx[:, 2 * b:2 * b + 2, h],
                                          bank_of("att_max", n)[:].rearrange("p (t k) -> p t k", t=2),
                                          AX.X, ALU.max).then_inc(sem["att_mx"], 1)
                    if n in EXPERT_AT:
                        expert_hidden(EXPERT_AT[n])
                        expert_add(EXPERT_AT[n])
                dve.wait_ge(sem["att_mx"], now("att_mx", 32))
                link(V.tensor_scalar(anm[:, :, 0, :], amx[:], -1.0, None, ALU.mult))
                V.scalar_tensor_tensor(anm[:, :, 1, :], amx[:], -1.0, anm[:, :, 0, :], ALU.mult,
                                       ALU.subtract).then_inc(sem["att_nm"], 1)
                expert_hidden(EX)
                for b in range(G):
                    dve.wait_ge(sem["att_pv"], now("att_pv", AH * (b + 1)))
                    heads_out(0, b, "att_pv", "att_o")
                dve.wait_ge(sem["final_ps"], now("final_ps", 1))
                dve.wait_ge(sem["moe_acc"], now("moe_acc", 8))
                V.tensor_tensor(res[:], moe[:], bank_of("final")[:].rearrange("p (t d) -> p t d", t=TT),
                                      ALU.add).then_inc(sem["result"], 1)


ROUTE_EXP = 150
COUNTS["loc_sum_cols"] = 16
del COUNTS["loc_sum_ps"]


_WEIGHTS = None


def kernel(**inputs):
    import concourse.bacc as _bacc
    from concourse.bass_utils import run_bass_kernel_spmd as _run

    f = {n: np.asarray(a) for n, a in inputs.items()}

    def g(n):
        return f[n]

    def spread(v):
        return np.broadcast_to(v, (P,) + v.shape)

    def chunks(v, off):
        return [v[off + o:off + o + P] if m == P else np.concatenate([v[off + o:off + o + m], v[off:off + P - m]])
                for o, m in HC]

    a = dict(consts())
    a["fw"] = np.stack([g("L0_attn_" + n) for n in ("q_w", "k_w", "v_w", "out_w")], 1)
    a["projT"] = np.tile(g("L0_attn_proj").T, (P // FD, 1))
    qs, ks = g("L0_ffn_q_scale"), g("L0_ffn_k_scale")
    cols = [g("L0_attn_q_b"), g("L0_attn_k_b")]
    for l in range(DEPTH):
        for s in (qs[l], ks[l]):
            cols.append(np.tile(s, 2))
            cols.append(np.tile(np.roll(s, LD // 2), 2))
    cols += [g("L0_ffn_ln_g")[l] for l in range(DEPTH)]
    cols += [g("L0_ffn_b2")[l] for l in range(DEPTH)]
    cols += [g("L0_ffn_b2")[0]]
    cols += [g("L0_ffn_ln_b")[l] for l in range(DEPTH)]
    cols += [g("L1_attn_bq"), g("L1_attn_bk")]
    a["cols"] = np.stack(cols, 1)
    a["rows"] = spread(np.stack([g("L0_attn_v_b"), g("L0_attn_out_b"), g("L0_attn_gamma"), g("L0_attn_beta"),
                                 g("L1_attn_bv"), g("L1_attn_bo")]))
    a["wqkv"] = g("L0_ffn_wqkv").transpose(1, 0, 2)
    a["wo"] = g("L0_ffn_wo").reshape(DEPTH, 4, P, D).transpose(2, 0, 1, 3)
    a["w1"] = g("L0_ffn_w1").transpose(1, 0, 2)
    b1 = g("L0_ffn_b1")
    a["b1"] = np.stack([c for l in range(DEPTH)
                        for pair in zip(chunks(b1[l], 0), chunks(b1[l], HID)) for c in pair], 1)
    w2 = g("L0_ffn_w2")
    a["w2"] = np.stack([np.stack([w2[l, o:o + P] if m == P else np.concatenate([w2[l, o:o + m], w2[l, :P - m]])
                                  for o, m in HC]) for l in range(DEPTH)]).transpose(2, 0, 1, 3)
    a["aw"] = np.stack([g("L1_attn_" + n).T for n in ("Wq", "Wk", "Wv", "Wo")], 1)
    a["wr"] = g("L1_ffn_Wr")
    a["rb"] = spread(g("L1_ffn_rb"))
    for n, e, s in (("mw1", "W1", "Ws1"), ("mw3", "W3", "Ws3")):
        a[n] = np.concatenate([g("L1_ffn_" + e), g("L1_ffn_" + s)[None]]).transpose(1, 0, 2)
    a["mw2"] = np.concatenate([g("L1_ffn_W2"), g("L1_ffn_Ws2")[None]]).reshape(EX + 1, 2, P, D).transpose(2, 0, 1, 3)

    nc = _bacc.Bacc("TRN2", target_bir_lowering=False, num_devices=1)
    arrays, w = {}, {}
    for n, v in a.items():
        v = np.ascontiguousarray(v)
        arrays["in_" + n] = v
        w[n] = nc.dram_tensor("in_" + n, v.shape, mybir.dt.from_np(v.dtype), kind="ExternalInput").ap()
    xs = np.ascontiguousarray(g("L0_attn_x"))
    arrays["in_x"] = xs
    flat = "(i b) (t p) d -> i p (b t) d"
    x = nc.dram_tensor("in_x", xs.shape, F32, kind="ExternalInput").ap()
    out = nc.dram_tensor("out", xs.shape, F32, kind="ExternalOutput").ap()
    x = x.rearrange("n s d -> (n s) d").rearrange("(i j p) d -> i p j d", j=TT, p=P)
    o = out.rearrange("n s d -> (n s) d").rearrange("(i j p) d -> i p j d", j=TT, p=P)
    build(nc, w, x, o)
    r = _run(nc, [arrays], core_ids=[0])
    return r.results[0]["out"]
```
